# Optimizing a Trainium2 kernel written in Bass

```python
import numpy as np
import jax
import jax.numpy as jnp

def _softmax(x, axis=-1):
    return jax.nn.softmax(x, axis=axis)

def _gelu(x):
    return jax.nn.gelu(x, approximate=True)

def _silu(x):
    return jax.nn.silu(x)

def _sigmoid(x):
    return jax.nn.sigmoid(x)

def _layernorm(x, axis=-1, eps=1e-05):
    m = jnp.mean(x, axis=axis, keepdims=True)
    v = jnp.var(x, axis=axis, keepdims=True)
    return (x - m) / jnp.sqrt(v + eps)

def _scatter_add(tgt, idx, src, axis=0):
    return tgt.at[idx].add(src)

def _segment_sum(src, seg, n):
    return jax.ops.segment_sum(src, seg, n)
kernel_name = 'mk_xattn_ffn_d1_seqx_r4_502e00'

def setup_inputs(seed: int=0):
    np.random.seed(seed)
    _w = jnp.asarray

    def _rec_inputs():
        import jax
        import jax.numpy as jnp
        _rk = jax.random.key(seed)
        x = 7.22e-05 + 1 * jax.random.normal(jax.random.fold_in(_rk, 1), (2, 1024, 256), jnp.float32)
        _lenS = 1024 - jax.random.randint(jax.random.fold_in(_rk, 7), (2,), 0, max(1, 1024 // 4) + 1, jnp.int32)
        _lenS2 = 154 - jax.random.randint(jax.random.fold_in(_rk, 8), (2,), 0, max(1, 154 // 4) + 1, jnp.int32)
        _ctx_1024P = jax.random.normal(jax.random.fold_in(_rk, 11), (2, 16, 256), jnp.float32)
        _ctx_1024c = jax.random.dirichlet(jax.random.fold_in(_rk, 511), 0.3 * jnp.ones((16,), jnp.float32), (2, 154))
        _ctx_1024t = jnp.einsum('bsk,bkd->bsd', _ctx_1024c, _ctx_1024P)
        _ctx_1024t = _ctx_1024t * jax.lax.rsqrt(jnp.mean(jnp.square(_ctx_1024t)) + 1e-12) * 0.953939
        ctx_1024 = -1.52775e-05 + 0.999936 * (_ctx_1024t + 0.3 * jax.random.normal(jax.random.fold_in(_rk, 611), (2, 154, 256), jnp.float32))
        _validS = jnp.arange(1024)[None, :] < _lenS[:, None]
        _validS2 = jnp.arange(154)[None, :] < _lenS2[:, None]
        _causal = jnp.tril(jnp.ones((1024, 1024), dtype=bool))
        mask_BxSxS2_bk0 = jnp.logical_not(jnp.broadcast_to(_validS2[:, None, :], (2, 1024, 154)))
        return (x, ctx_1024, mask_BxSxS2_bk0)
    x, ctx_1024, mask_BxSxS2_bk0 = _rec_inputs()

    def _L0_xattn_setup():
        import jax, jax.numpy as jnp
        import numpy as np
        B, TQ, TK, D, ATTN = (16, 128, 512, 256, 256)
        key = jax.random.key(seed)
        k1, k2, k3, k4 = jax.random.split(key, 4)
        dec_out = jax.random.normal(k1, (B, TQ, D), dtype=jnp.float32)
        enc_out = jax.random.normal(k2, (B, TK, D), dtype=jnp.float32)
        enc_mask = jax.random.randint(k3, (B, TQ, TK), 0, 2) == 1
        W_attn = jax.random.normal(k4, (ATTN, 2 * D), dtype=jnp.float32) * (np.sqrt(6.0) * np.sqrt(6.0 / (2 * D + ATTN)))
        return {'dec_out': dec_out, 'enc_out': enc_out, 'enc_mask': enc_mask, 'W_attn': W_attn}
    _L0_xattn_all = _L0_xattn_setup()
    _L0_xattn_in = {k: v for k, v in _L0_xattn_all.items() if k in ('W_attn',)}
    del _L0_xattn_all

    def _L0_ffn_setup():
        import jax, jax.numpy as jnp
        import numpy as np
        D = 256
        H = 256
        E = 8
        K = 2
        I = 2 * 256
        ROUTE_SCALE = 1.0
        key = jax.random.key(seed)
        ks = jax.random.split(key, 12)
        s = lambda *sh: 1.0 / np.sqrt(sh[-1])
        return {'x': jax.random.normal(ks[0], (1, 512, D), jnp.float32), 'gate_w': jax.random.normal(ks[1], (E, D), jnp.float32) * s(E, D), 'w1': jax.random.normal(ks[2], (E, H, D), jnp.float32) * s(H, D), 'b1': jax.random.normal(ks[3], (E, H), jnp.float32) * 0.01, 'w2': jax.random.normal(ks[4], (E, D, H), jnp.float32) * s(D, H), 'b2': jax.random.normal(ks[5], (E, D), jnp.float32) * 0.01, 'w3': jax.random.normal(ks[6], (E, H, D), jnp.float32) * s(H, D), 'b3': jax.random.normal(ks[7], (E, H), jnp.float32) * 0.01, 'sw1': jax.random.normal(ks[8], (I, D), jnp.float32) * s(I, D), 'sw2': jax.random.normal(ks[9], (I, D), jnp.float32) * s(I, D), 'sw3': jax.random.normal(ks[10], (D, I), jnp.float32) * s(D, I)}
    _L0_ffn_all = _L0_ffn_setup()
    _L0_ffn_in = {k: v for k, v in _L0_ffn_all.items() if k in ('gate_w', 'w1', 'b1', 'w2', 'b2', 'w3', 'b3', 'sw1', 'sw2', 'sw3')}
    del _L0_ffn_all
    return {'x': x, 'ctx_1024': ctx_1024, 'mask_BxSxS2_bk0': mask_BxSxS2_bk0, 'L0_xattn_W_attn': _L0_xattn_in['W_attn'], 'L0_ffn_gate_w': _L0_ffn_in['gate_w'], 'L0_ffn_w1': _L0_ffn_in['w1'], 'L0_ffn_b1': _L0_ffn_in['b1'], 'L0_ffn_w2': _L0_ffn_in['w2'], 'L0_ffn_b2': _L0_ffn_in['b2'], 'L0_ffn_w3': _L0_ffn_in['w3'], 'L0_ffn_b3': _L0_ffn_in['b3'], 'L0_ffn_sw1': _L0_ffn_in['sw1'], 'L0_ffn_sw2': _L0_ffn_in['sw2'], 'L0_ffn_sw3': _L0_ffn_in['sw3']}

def reference(x, ctx_1024, mask_BxSxS2_bk0, L0_xattn_W_attn, L0_ffn_gate_w, L0_ffn_w1, L0_ffn_b1, L0_ffn_w2, L0_ffn_b2, L0_ffn_w3, L0_ffn_b3, L0_ffn_sw1, L0_ffn_sw2, L0_ffn_sw3):
    import jax
    import jax.numpy as jnp

    def _L0_xattn_ref(dec_out, enc_out, enc_mask, W_attn):
        import jax, jax.numpy as jnp
        import numpy as np
        B, TQ, TK, D, ATTN = (16, 128, 512, 256, 256)
        attn = jnp.einsum('bqd,bkd->bqk', dec_out, enc_out)
        attn = jnp.where(enc_mask, -jnp.inf, attn)
        attn = jax.nn.softmax(attn, axis=2)
        context = jnp.einsum('bqk,bkd->bqd', attn, enc_out)
        cat = jnp.concatenate([context, dec_out], axis=2)
        output = jnp.einsum('bqf,af->bqa', cat, W_attn)
        return output

    def _L0_ffn_ref(x, gate_w, w1, b1, w2, b2, w3, b3, sw1, sw2, sw3):
        import jax, jax.numpy as jnp
        import numpy as np
        D = 256
        H = 256
        E = 8
        K = 2
        I = 2 * 256
        ROUTE_SCALE = 1.0
        B, S, _ = x.shape
        xt = x.reshape(-1, D)
        logits = xt @ gate_w.T
        scores = jax.nn.softmax(logits.astype(jnp.float32), axis=-1)
        top_vals, idx = jax.lax.top_k(scores, K)
        weights = jnp.take_along_axis(scores, idx, axis=1).astype(x.dtype) * ROUTE_SCALE
        xs = xt[:, None, :] * weights[:, :, None]
        y = jnp.zeros_like(xt)
        for e in range(E):
            mask = (idx == e).astype(x.dtype)
            h = jax.nn.silu(jnp.einsum('tkd,hd->tkh', xs, w1[e]) + b1[e])
            x2 = jnp.einsum('tkh,dh->tkd', h, w2[e]) + b2[e]
            x3 = jnp.einsum('tkd,hd->tkh', xs, w3[e]) + b3[e]
            y = y + jnp.sum(x2 * x3 * mask[:, :, None], axis=1)
        z = jax.nn.silu(xt @ sw1.T) * (xt @ sw2.T) @ sw3.T
        return (y + z).reshape(B, S, D)
    x = x + _L0_xattn_ref(_layernorm(x, axis=-1), ctx_1024, mask_BxSxS2_bk0, L0_xattn_W_attn)
    x = x + _L0_ffn_ref(_layernorm(x, axis=-1), L0_ffn_gate_w, L0_ffn_w1, L0_ffn_b1, L0_ffn_w2, L0_ffn_b2, L0_ffn_w3, L0_ffn_b3, L0_ffn_sw1, L0_ffn_sw2, L0_ffn_sw3)
    return x

_drawn_inputs = setup_inputs


def setup_inputs(seed=0):
    import zlib

    import numpy as np

    out = dict(_drawn_inputs(seed))
    spreads = {}
    factors = {'L0_ffn_gate_w': 2.896, 'L0_ffn_b1': 64.0, 'L0_ffn_b2': 37.698, 'L0_ffn_b3': 64.0}
    for name, (base, spread) in spreads.items():
        noise = np.random.default_rng([zlib.crc32(name.encode()), seed]).standard_normal(out[name].shape)
        drawn = base * np.exp(spread * noise) if base else spread * noise
        out[name] = jnp.asarray(drawn.astype(out[name].dtype))
    for name, factor in factors.items():
        out[name] = (out[name] * factor).astype(out[name].dtype)
    return out
```

```python
from contextlib import ExitStack

import concourse.bass as bass
from concourse import mybir

F32 = mybir.dt.float32
F32R = mybir.dt.float32r
BF16 = mybir.dt.bfloat16
I32 = mybir.dt.int32
U8 = mybir.dt.uint8
ALU = mybir.AluOpType
ACT = mybir.ActivationFunctionType
X = mybir.AxisListType.X

P = 128
B, S, D = 2, 1024, 256
KEYS = 154
T = B * S
NT = T // P
TB = NT // B
DC = D // P
NE, TOP = 8, 2
H = 256
FI = 512
REGION = T + P
FILLER = NE * REGION
ROW = D + 4
NCONST = 17
MAXT = (T * TOP + NE * (P - 1)) // P
SKIP = 1 << 20
EPS = 1e-5
NEG = -3.0e38


def bass_xattn_moe(nc, x, enc_t, mask, w_ctx, w_dec, gate_t, sw12, sw3, w13, w2, bias, out):
    ctx = ExitStack()
    with ctx:
        def sb(name, shape, dt=F32):
            return ctx.enter_context(nc.sbuf_tensor(name, shape, dt))

        def bank(name):
            return ctx.enter_context(nc.psum_tensor(name, [P, 512], F32))

        def sem(name):
            return ctx.enter_context(nc.semaphore(name))

        sorted_rows = nc.dram_tensor("sorted_rows", [FILLER + P, ROW], F32, kind="Internal").ap()
        expert_out = nc.dram_tensor("expert_out", [TOP * T, D], F32, kind="Internal").ap()

        x_all = sb("x_all", [P, NT, D])
        w13_hi = sb("w13_hi", [P, NE, DC, 2 * H], F32R)
        w13_lo = sb("w13_lo", [P, NE, DC, 2 * H], F32R)
        w2_hi = sb("w2_hi", [P, NE, DC, D], F32R)
        w2_lo = sb("w2_lo", [P, NE, DC, D], F32R)
        sw12_hi = sb("sw12_hi", [P, DC, 2 * FI], F32R)
        sw12_lo = sb("sw12_lo", [P, DC, 2 * FI], F32R)
        sw3_hi = sb("sw3_hi", [P, FI // P, D], F32R)
        sw3_lo = sb("sw3_lo", [P, FI // P, D], F32R)
        bias_all = sb("bias_all", [P, NE, 3 * H])
        stage = sb("stage", [P, 2, 1024])
        gate_raw = sb("gate_raw", [P, DC, NE])
        gate_hi = sb("gate_hi", [P, DC, NE], F32R)
        gate_lo = sb("gate_lo", [P, DC, NE], F32R)
        mask_sb = sb("mask_sb", [P, NT, KEYS], U8)
        def att(t, e):
            return t[:, e, :, :].rearrange("p c n -> p (c n)")
        encT_hi = att(w13_hi, 7).rearrange("p (b c k) -> p b c k", b=B, c=DC)
        encT_lo = att(w13_lo, 7).rearrange("p (b c k) -> p b c k", b=B, c=DC)
        encW_hi = att(w13_hi, 6).rearrange("p (b c n) -> p b c n", b=B, c=2)
        encW_lo = att(w13_lo, 6).rearrange("p (b c n) -> p b c n", b=B, c=2)
        wdec_hi = w2_hi[:, 7, :, :]
        wdec_lo = w2_lo[:, 7, :, :]

        ident = sb("ident", [P, P])
        earlier = sb("earlier", [P, P], BF16)
        ones = sb("ones", [P, P], BF16)
        nhalf = sb("nhalf", [P, 1])
        desc = sb("desc", [P, 2, NE])
        dest_i = sb("dest_i", [P, NT, TOP], I32)
        fill_blk = sb("fill_blk", [P, ROW])
        next_row = sb("next_row", [P, NE])
        base_row = sb("base_row", [1, NE])
        m128 = sb("m128", [1, NE, NT])
        upto = sb("upto", [1, NE, NE])

        st6 = sb("st6", [P, 2, 6])
        mv = sb("mv", [P, 2, 2])
        ve = sb("ve", [P, 2])
        rstd = sb("rstd", [P, 2])
        xn = sb("xn", [P, 2, D])
        xT_hi = sb("xT_hi", [P, DC, P], F32R)
        xT_lo = sb("xT_lo", [P, DC, P], F32R)
        smk = sb("smk", [P, KEYS])
        negmax = sb("negmax", [P, 1])
        probs = sb("probs", [P, 2, D])
        psum_p = sb("psum_p", [P, 2])
        prcp = sb("prcp", [P, 2])
        pT_hi = sb("pT_hi", [P, 2, P], F32R)
        pT_lo = sb("pT_lo", [P, 2, P], F32R)
        xn2 = sb("xn2", [P, 4, D])
        x2T_hi = sb("x2T_hi", [P, DC, P], F32R)
        x2T_lo = sb("x2T_lo", [P, DC, P], F32R)
        tanh_g = sb("tanh_g", [P, FI])
        gsil = sb("gsil", [P, FI])
        hid = sb("hid", [P, FI])
        hT_hi = sb("hT_hi", [P, 4, P], F32R)
        hT_lo = sb("hT_lo", [P, 4, P], F32R)
        logit = sb("logit", [P, 2, NE])
        rmax = sb("rmax", [P, 2])
        ex = sb("ex", [P, 2, NE])
        rsum = sb("rsum", [P, 2])
        rrcp = sb("rrcp", [P, 2])
        score = sb("score", [P, 2, NE])
        cand = sb("cand", [P, 2, NE])
        first = sb("first", [P, 2])
        hot = sb("hot", [P, TOP, 2, NE])
        wgt = sb("wgt", [P, TOP, 2])
        rest = sb("rest", [P, 2, NE])
        member = sb("member", [P, 2, NE], BF16)
        rank = sb("rank", [P, 2, NE])
        rsel = sb("rsel", [P, TOP, 2, NE])
        pos_i = sb("pos_i", [P, TOP, 2], I32)
        rows = sb("rows", [P, 4, ROW])
        cnt = sb("cnt", [1, NE])
        over = sb("over", [1, NE, NT])
        ntile = sb("ntile", [1, NE])
        cumx = sb("cumx", [1, NE, NE])
        cum = sb("cum", [1, NE])
        te = sb("te", [1, MAXT])
        tstart = sb("tstart", [1, MAXT])
        trow = sb("trow", [1, MAXT])
        trow2 = sb("trow2", [1, MAXT])
        te_i = sb("te_i", [1, MAXT], I32)
        trow_i = sb("trow_i", [1, MAXT], I32)
        fill_i = sb("fill_i", [1, NE], I32)
        tile_no = sb("tile_no", [1, MAXT, NE])
        ended = gsil[0:1, 0:MAXT * NE].rearrange("p (j e) -> p j e", e=NE)
        rin = rows
        eT_hi = [x2T_hi[:, :, :], xT_hi[:, :, :]]
        eT_lo = [x2T_lo[:, :, :], xT_lo[:, :, :]]
        ehT_hi = [pT_hi[:, :, :], hT_hi[:, 0:2, :]]
        ehT_lo = [pT_lo[:, :, :], hT_lo[:, 0:2, :]]
        u13 = [tanh_g[:, :], gsil[:, :], hid[:, :], stage[:, 0, 0:512]]
        dest_row = sb("dest_row", [P, 4], I32)
        ehid = xn
        yb = probs
        yout = [xn2[:, 0, :], xn2[:, 1, :], stage[:, 1, 0:256], stage[:, 1, 256:512]]

        psX = bank("psX")
        psX2 = bank("psX2")
        psPT = bank("psPT")
        psHT = bank("psHT")
        psS = bank("psS")
        psG = bank("psG")
        psU = bank("psU")
        psO = bank("psO")
        psXe, psHe = psX, psHT
        psUe = [psG, psU]
        psYe = [psO, psS]

        s_const = sem("constants_made")
        s_gh = sem("gate_hi")
        s_x = [sem("x_pair0"), sem("x_rest")]
        s_mask = sem("mask_loaded")
        s_gate = sem("gate_loaded")
        s_bias = sem("bias_loaded")
        s_ld = [sem("stage0_loaded"), sem("stage1_loaded")]
        s_shi = sem("setup_hi")
        s_slo = sem("setup_lo")
        s_pad = sem("enc_padded")
        s_ehi = sem("expert_w_hi")
        s_elo = sem("expert_w_lo")
        s_lhi = sem("late_w_hi")
        s_llo = sem("late_w_lo")
        s_ew = sem("encW_product")
        s_ewh = sem("encW_hi")
        s_ewl = sem("encW_lo")
        s_bn1, s_mv1, s_ve1, s_rs1, s_xn = sem("ln1_stats"), sem("ln1_mv"), sem("ln1_ve"), sem("ln1_rstd"), sem("xn_ready")
        s_bn2, s_mv2, s_ve2, s_rs2, s_xn2 = sem("ln2_stats"), sem("ln2_mv"), sem("ln2_ve"), sem("ln2_rstd"), sem("xn2_ready")
        s_t1, s_xh, s_xl = sem("xT_psum"), sem("xT_hi_ready"), sem("xT_lo_ready")
        s_s, s_sm, s_nm, s_ex, s_rc, s_p = sem("scores"), sem("scores_masked"), sem("negmax_ready"), sem("exp_done"), sem("prcp_ready"), sem("probs_ready")
        s_tp, s_ph, s_pl = sem("pT_psum"), sem("pT_hi_ready"), sem("pT_lo_ready")
        s_o, s_x1 = sem("attn_out"), sem("x1_ready")
        s_t2, s_x2h, s_x2l = sem("x2T_psum"), sem("x2T_hi_ready"), sem("x2T_lo_ready")
        s_gl, s_lg = sem("gate_logits"), sem("logits_copied")
        s_g, s_th, s_gs = sem("ffn_g"), sem("tanh_done"), sem("gsil_ready")
        s_u, s_h = sem("ffn_u"), sem("hidden_ready")
        s_ht, s_hh, s_hl = sem("hT_psum"), sem("hT_hi_ready"), sem("hT_lo_ready")
        s_z, s_zd = sem("ffn_z"), sem("z_added")
        s_rt = sem("route_step")
        s_lc = sem("route_shifted")
        s_re = sem("route_exp")
        s_mem = sem("members_ready")
        s_rk = sem("ranks")
        s_rr = sem("ranks_read")
        s_wr = sem("weights_ready")
        s_pos = sem("pos_ready")
        s_row = sem("rows_scaled")
        s_sc = [sem(f"rows_scattered{k}") for k in range(4)]
        s_tb = sem("table_step")
        s_tab = sem("table_ready")
        s_fill = sem("filler_written")
        s_rin = [sem(f"rin{k}_loaded") for k in range(4)]
        s_te, s_eh, s_el = sem("eT_psum"), sem("eT_hi_ready"), sem("eT_lo_ready")
        s_up, s_ub, s_si = sem("e_up"), sem("e_biased"), sem("e_silu")
        s_the, s_heh, s_hel = sem("ehT_psum"), sem("ehT_hi_ready"), sem("ehT_lo_ready")
        s_ix = sem("dest_rows_copied")
        s_dn, s_yb, s_yo = sem("e_down"), sem("e_y_biased"), sem("e_y_ready")
        s_ys = [sem(f"y_scattered{k}") for k in range(4)]
        s_c = [sem(f"comb{k}_loaded") for k in range(3)]
        s_c1, s_c2 = sem("comb_first"), sem("comb_done")
        s_out = sem("out_stored")

        s_pv, s_pp, s_pg = sem("passed_dve"), sem("passed_pe"), sem("passed_pool")

        block = ctx.enter_context(nc.Block())

        def apart(engine, passed):
            engine.sem_inc(passed, 1)

        def past(i, n):
            return not isinstance(i, int) or i >= n

        NSET = 5
        wctx_hi = hT_hi[:, :, :].rearrange("p a b -> p (a b)").rearrange("p (c n) -> p c n", c=DC)
        wctx_lo = hT_lo[:, :, :].rearrange("p a b -> p (a b)").rearrange("p (c n) -> p c n", c=DC)

        def setup_parts(n):
            raw = stage[:, n % 2, :]
            if n == 0:
                r = raw[:, 0:B * DC * KEYS].rearrange("p (b c k) -> p b c k", b=B, c=DC)
                return [(r[:, b], encT_hi[:, b, :, 0:KEYS], encT_lo[:, b, :, 0:KEYS]) for b in range(B)]
            if n == 1:
                return [(raw[:, 0:512].rearrange("p (c n) -> p c n", c=DC), wctx_hi, wctx_lo),
                        (raw[:, 512:1024].rearrange("p (c n) -> p c n", c=DC), wdec_hi, wdec_lo)]
            if n < 4:
                return [(raw, sw12_hi[:, n - 2, :], sw12_lo[:, n - 2, :])]
            return [(raw, sw3_hi[:, :, :].rearrange("p c n -> p (c n)"), sw3_lo[:, :, :].rearrange("p c n -> p (c n)"))]

        def w13_raw():
            return stage[:, 1, :]

        def w2_raw():
            return stage[:, 0, 0:DC * D]

        def flat(t, e):
            return t[:, bass.ds(e, 1), :, :].rearrange("p a c n -> p (a c n)")

        def comb(c):
            return bias_all[:, :, :].rearrange("p e n -> p (e n)").rearrange("p (k s t d) -> p k s t d", k=3, s=TOP, t=4)[:, c % 3]

        @block.sync
        def _(sp):
            xv = x.rearrange("b (p t) d -> p b t d", t=TB)
            sp.dma_start(x_all[:, 0:2, :], xv[:, 0, 0:2, :]).then_inc(s_x[0], 16)
            sp.dma_start(stage[:, 0, 0:B * DC * KEYS].rearrange("p (b c k) -> p b c k", b=B, c=DC),
                         enc_t.rearrange("b (c p) k -> p b c k", p=P)).then_inc(s_ld[0], 16)
            sp.dma_start(stage[:, 1, :].rearrange("p (w c n) -> p w c n", w=2, c=DC)[:, 0], w_ctx.rearrange("(c p) n -> p c n", p=P)).then_inc(s_ld[1], 16)
            sp.dma_start(stage[:, 1, :].rearrange("p (w c n) -> p w c n", w=2, c=DC)[:, 1], w_dec.rearrange("(c p) n -> p c n", p=P)).then_inc(s_ld[1], 16)
            for c in range(DC):
                sp.wait_ge(s_slo, c + 1)
                sp.dma_start(stage[:, c, :], sw12[c * P:(c + 1) * P, :]).then_inc(s_ld[c], 16)
            sp.wait_ge(s_slo, 3)
            sp.dma_start(stage[:, 0, :].rearrange("p (c n) -> p c n", n=D), sw3.rearrange("(c p) n -> p c n", p=P)).then_inc(s_ld[0], 16)

            def load_w13(e):
                sp.dma_start(w13_raw().rearrange("p (c n) -> p c n", c=DC), w13.rearrange("e (c p) n -> p e c n", p=P)[:, bass.ds(e, 1)].rearrange("p a c n -> p (a c) n")).then_inc(s_ld[1], 16)

            def load_w2(e):
                sp.dma_start(w2_raw().rearrange("p (c n) -> p c n", c=DC), w2.rearrange("e (c p) n -> p e c n", p=P)[:, bass.ds(e, 1)].rearrange("p a c n -> p (a c) n")).then_inc(s_ld[0], 16)

            sp.wait_ge(s_slo, 4)
            load_w13(0)
            sp.wait_ge(s_slo, 5)
            load_w2(0)
            with sp.Fori(1, 6) as e:
                sp.wait_ge(s_elo, 2 * e - 1)
                load_w13(e)
                sp.wait_ge(s_elo, 2 * e)
                load_w2(e)
            sp.dma_start(bias_all[:, :, :].rearrange("p e n -> p (e n)"), bias.rearrange("e n -> (e n)").partition_broadcast(P)).then_inc(s_bias, 16)
            for e in (6, 7):
                if e == 6:
                    sp.wait_ge(s_elo, 11)
                else:
                    sp.wait_ge(s_llo, 1)
                load_w13(e)
                if e == 6:
                    sp.wait_ge(s_elo, 12)
                else:
                    sp.wait_ge(s_llo, 2)
                load_w2(e)

            sp.wait_ge(s_tab, 3)
            for e in range(NE):
                r = sp.value_load(fill_i[0:1, e:e + 1], min_val=e * REGION, max_val=e * REGION + T)
                sp.dma_start(sorted_rows[bass.ds(r, P), :], fill_blk[:]).then_inc(s_fill, 16)
            sp.dma_start(sorted_rows[FILLER:FILLER + P, :], fill_blk[:]).then_inc(s_fill, 16)
            sp.wait_ge(s_fill, 16 * (NE + 1))
            for k in range(4):
                sp.wait_ge(s_sc[k], 16 * NT // 2)

            def load_rows(j, k, reuse):
                if reuse is not None:
                    sp.wait_ge(s_ix, reuse)
                r = sp.value_load(trow_i[0:1, bass.ds(j, 1)], min_val=0, max_val=FILLER)
                sp.dma_start(rin[:, k, :], sorted_rows[bass.ds(r, P), :]).then_inc(s_rin[k], 16)

            for j in range(4):
                load_rows(j, j, None)
            with sp.Fori(1, 9) as q:
                for k in range(4):
                    load_rows(4 * q + k, k, 4 * q + k - 3)
            for j in range(36, MAXT):
                load_rows(j, j % 4, j - 3)

            for k in range(4):
                sp.wait_ge(s_ys[k], 16 * len(range(k, MAXT, 4)))
            yv = expert_out.rearrange("(s b p t) d -> p s b t d", s=TOP, b=B, t=TB)
            ov = out.rearrange("b (p t) d -> p b t d", t=TB)

            def load_comb(c):
                for s in range(TOP):
                    sp.dma_start(comb(c)[:, s], yv[:, s, c // 2, (c % 2) * 4:(c % 2) * 4 + 4, :]).then_inc(s_c[c % 3], 16)

            sp.wait_ge(s_yb, MAXT)
            for c in range(3):
                load_comb(c)
            sp.wait_ge(s_c2, 1)
            load_comb(3)
            for c in range(4):
                sp.wait_ge(s_c2, c + 1)
                sp.dma_start(ov[:, c // 2, (c % 2) * 4:(c % 2) * 4 + 4, :], x_all[:, 4 * c:4 * c + 4, :]).then_inc(s_out, 16)
            sp.wait_ge(s_out, 64)

        @block.tensor
        def _(pe):
            def three(o, lh, ll, rh, rl, start, stop):
                pe.matmul(o, lh, rh, start=start, stop=False)
                pe.matmul(o, lh, rl, start=False, stop=False)
                return pe.matmul(o, ll, rh, start=False, stop=stop)

            pe.wait_ge(s_slo, 2)
            pe.wait_ge(s_pad, 2)
            for b in range(B):
                for k in range(2):
                    o = [psG, psU][b][:, k * D:(k + 1) * D]
                    for c in range(DC):
                        ks = slice(k * P, (k + 1) * P)
                        mm = three(o, encT_hi[:, b, c, ks], encT_lo[:, b, c, ks], wctx_hi[:, c], wctx_lo[:, c], c == 0, c == DC - 1)
                mm.then_inc(s_ew, 1)
            pe.wait_ge(s_const, NCONST)
            pe.wait_ge(s_pad, 3)
            pe.wait_ge(s_ewl, 2)

            def step(i, u, pair, b, attn=True, mid=True, tail=True):
                late = past(i, 2)
                if attn:
                    pe.wait_ge(s_xn, i + 1)
                    if past(i, 3):
                        pe.wait_ge(s_zd, i - 2)
                    for c in range(DC):
                        mm = pe.transpose(psX[:, c * P:(c + 1) * P], xn[:, u % 2, c * P:(c + 1) * P], ident[:])
                    mm.then_inc(s_t1, 1)
                if tail:
                    pe.wait_ge(s_h, i - 1)
                    for c in range(4):
                        mm = pe.transpose(psHT[:, c * P:(c + 1) * P], hid[:, c * P:(c + 1) * P], ident[:])
                    mm.then_inc(s_ht, 1)
                if attn:
                    pe.wait_ge(s_xl, i + 1)
                    if past(i, 1):
                        pe.wait_ge(s_sm, i)
                    for c in range(DC):
                        mm = three(psS[:, 0:KEYS], xT_hi[:, c], xT_lo[:, c], encT_hi[:, b, c, 0:KEYS], encT_lo[:, b, c, 0:KEYS], c == 0, c == DC - 1)
                    mm.then_inc(s_s, 1)
                if tail:
                    pe.wait_ge(s_hl, i - 1)
                    for c in range(4):
                        mm = three(psX[:, D:2 * D], hT_hi[:, c], hT_lo[:, c], sw3_hi[:, c], sw3_lo[:, c], c == 0, c == 3)
                    mm.then_inc(s_z, 1)
                if mid:
                    pe.wait_ge(s_xn2, i)
                    if late:
                        pe.wait_ge(s_lg, i - 1)
                    for c in range(DC):
                        mm = pe.transpose(psX2[:, c * P:(c + 1) * P], xn2[:, (u - 1) % 4, c * P:(c + 1) * P], ident[:])
                    mm.then_inc(s_t2, 1)
                if attn:
                    if past(i, 1):
                        pe.wait_ge(s_x1, i)
                    for c in range(DC):
                        three(psO[:, 0:D], xT_hi[:, c], xT_lo[:, c], wdec_hi[:, c], wdec_lo[:, c], c == 0, False)
                if mid:
                    pe.wait_ge(s_x2l, i)
                    for c in range(DC):
                        mm = three(psX2[:, D:D + NE], x2T_hi[:, c], x2T_lo[:, c], gate_hi[:, c], gate_lo[:, c], c == 0, c == DC - 1)
                    mm.then_inc(s_gl, 1)
                    if late:
                        pe.wait_ge(s_gs, i - 1)
                    for c in range(DC):
                        mm = three(psG[:, :], x2T_hi[:, c], x2T_lo[:, c], sw12_hi[:, c, 0:FI], sw12_lo[:, c, 0:FI], c == 0, c == DC - 1)
                    mm.then_inc(s_g, 1)
                if attn:
                    pe.wait_ge(s_p, i + 1)
                    if u % 2 == 0 and past(i, 4):
                        pe.wait_ge(s_rr, pair - 1)
                    for c in range(2):
                        mm = pe.transpose(psPT[:, c * P:(c + 1) * P], probs[:, u % 2, c * P:(c + 1) * P], ident[:])
                    mm.then_inc(s_tp, 1)
                if mid:
                    if late:
                        pe.wait_ge(s_h, i - 1)
                    for c in range(DC):
                        mm = three(psU[:, :], x2T_hi[:, c], x2T_lo[:, c], sw12_hi[:, c, FI:2 * FI], sw12_lo[:, c, FI:2 * FI], c == 0, c == DC - 1)
                    mm.then_inc(s_u, 1)
                if attn:
                    pe.wait_ge(s_pl, i + 1)
                    if u % 2 == 1 and past(i, 3):
                        ranks(pair)
                if attn:
                    for c in range(2):
                        mm = three(psO[:, 0:D], pT_hi[:, c], pT_lo[:, c], encW_hi[:, b, c], encW_lo[:, b, c], False, c == 1)
                    mm.then_inc(s_o, 1)

            def ranks(n):
                pe.wait_ge(s_mem, n)
                m0, m1 = member[:, 0, :], member[:, 1, :]
                pe.matmul(psPT[:, 256:264], earlier[:], m0, start=True, stop=True)
                pe.matmul(psPT[:, 264:272], earlier[:], m1, start=True, stop=False)
                pe.matmul(psPT[:, 264:272], ones[:], m0, start=False, stop=True)
                pe.matmul(psPT[:, 272:280], ones[:], m0, start=True, stop=False)
                pe.matmul(psPT[:, 272:280], ones[:], m1, start=False, stop=True).then_inc(s_rk, 1)

            step(0, 0, 0, 0, mid=False, tail=False)
            pe.wait_ge(s_slo, 5)
            pe.wait_ge(s_gate, 17)
            step(1, 1, 0, 0, tail=False)
            for i in range(2, TB):
                step(i, i % 4, i // 2, 0)
            with pe.Fori(TB // 4, NT // 4) as q:
                for u in range(4):
                    step(4 * q + u, u, 2 * q + u // 2, 1)
            step(16, 0, 8, 1, attn=False)
            ranks(NT // 2)
            step(17, 1, 8, 1, attn=False, mid=False)

            pe.wait_ge(s_llo, 4)
            pe.wait_ge(s_tab, 3)

            def estep(i, u, q, new=True, up=True, down=True):
                if new:
                    k = u % 4
                    pe.wait_ge(s_rin[k], 16 * (q + 1))
                    if past(i, 1):
                        pe.wait_ge(s_el, i)
                    for c in range(DC):
                        mm = pe.transpose(psXe[:, c * P:(c + 1) * P], rin[:, k, c * P:(c + 1) * P], ident[:])
                    mm.then_inc(s_te, 1)
                if down:
                    pe.wait_ge(s_si, i - 2)
                    for c in range(DC):
                        mm = pe.transpose(psHe[:, c * P:(c + 1) * P], ehid[:, (u - 3) % 2, c * P:(c + 1) * P], ident[:])
                    mm.then_inc(s_the, 1)
                if up:
                    pe.wait_ge(s_el, i)
                    if past(i, 3):
                        pe.wait_ge(s_ub, i - 2)
                    apart(pe, s_pp)
                    k = (u - 1) % 2
                    e = pe.value_load(te_i[0:1, bass.ds(i - 1, 1)], min_val=0, max_val=NE - 1)
                    wh = w13_hi[:, bass.ds(e, 1)].rearrange("p a c n -> p (a c) n")
                    wl = w13_lo[:, bass.ds(e, 1)].rearrange("p a c n -> p (a c) n")
                    for c in range(DC):
                        mm = three(psUe[k][:, :], eT_hi[k][:, c], eT_lo[k][:, c], wh[:, c], wl[:, c], c == 0, c == DC - 1)
                    mm.then_inc(s_up, 1)
                if down:
                    pe.wait_ge(s_hel, i - 2)
                    if past(i, 5):
                        pe.wait_ge(s_yb, i - 4)
                    apart(pe, s_pp)
                    k = (u - 3) % 2
                    e = pe.value_load(te_i[0:1, bass.ds(i - 3, 1)], min_val=0, max_val=NE - 1)
                    wh = w2_hi[:, bass.ds(e, 1)].rearrange("p a c n -> p (a c) n")
                    wl = w2_lo[:, bass.ds(e, 1)].rearrange("p a c n -> p (a c) n")
                    for c in range(DC):
                        mm = three(psYe[k][:, 0:D], ehT_hi[k][:, c], ehT_lo[k][:, c], wh[:, c], wl[:, c], c == 0, c == DC - 1)
                    mm.then_inc(s_dn, 1)

            for i in range(8):
                estep(i, i % 4, i // 4, up=i >= 1, down=i >= 3)
            with pe.Fori(2, MAXT // 4) as q:
                for u in range(4):
                    estep(4 * q + u, u, q)
            for i in range(MAXT // 4 * 4, MAXT + 3):
                estep(i, i % 4, i // 4, new=i < MAXT, up=i - 1 < MAXT)

        @block.scalar
        def _(act):
            xv = x.rearrange("b (p t) d -> p b t d", t=TB)
            act.dma_start(gate_raw[:], gate_t.rearrange("(c p) e -> p c e", p=P)).then_inc(s_gate, 16)
            act.dma_start(mask_sb[:, :, :].rearrange("p (b t) k -> p b (t k)", b=B), mask.rearrange("b (p t) k -> p b (t k)", t=TB)).then_inc(s_mask, 16)
            act.dma_start(x_all[:, 2:TB, :], xv[:, 0, 2:TB, :]).then_inc(s_x[1], 16)
            act.dma_start(x_all[:, TB:NT, :], xv[:, 1]).then_inc(s_x[1], 16)
            for n in range(NSET):
                act.wait_ge(s_ld[n % 2], [16, 32, 32, 48, 48][n])
                for raw, hi, _ in setup_parts(n):
                    mm = act.activation(hi, raw, ACT.Copy)
                mm.then_inc(s_shi, 1)
                if n == 1:
                    for b in range(B):
                        act.wait_ge(s_ew, b + 1)
                        act.activation(encW_hi[:, b].rearrange("p c n -> p (c n)"), [psG, psU][b][:, :], ACT.Copy).then_inc(s_ewh, 1)

            def evac(done, t, out, ps, ready):
                act.wait_ge(done, t)
                act.activation(out, ps, ACT.Copy).then_inc(ready, 1)

            def step(i, u, pair, attn=True, mid=True, tail=True):
                if attn:
                    evac(s_t1, i + 1, xT_hi[:, :, :], psX[:, 0:D].rearrange("p (c n) -> p c n", c=DC), s_xh)
                if tail:
                    evac(s_ht, i - 1, hT_hi[:, :, :], psHT[:, :].rearrange("p (c n) -> p c n", c=4), s_hh)
                if attn:
                    act.wait_ge(s_nm, i + 1)
                    if past(i, 2):
                        act.wait_ge(s_tp, i - 1)
                    act.activation(probs[:, u % 2, 0:KEYS], smk[:], ACT.Exp, bias=negmax[:, 0:1],
                                   accum_out=psum_p[:, u % 2:u % 2 + 1]).then_inc(s_ex, 1)
                if mid:
                    evac(s_t2, i, x2T_hi[:, :, :], psX2[:, 0:D].rearrange("p (c n) -> p c n", c=DC), s_x2h)
                    act.wait_ge(s_g, i)
                    if past(i, 2):
                        act.wait_ge(s_gs, i - 1)
                    act.activation(tanh_g[:], psG[:, :], ACT.Tanh, scale=0.5).then_inc(s_th, 1)
                if attn:
                    evac(s_tp, i + 1, pT_hi[:, :, :], psPT[:, 0:256].rearrange("p (c n) -> p c n", c=2), s_ph)
                if mid and u % 2 == 0:
                    act.wait_ge(s_lc, pair)
                    act.activation(ex[:, :, :], ex[:, :, :], ACT.Exp).then_inc(s_re, 1)

            step(0, 0, 0, mid=False, tail=False)
            step(1, 1, 0, tail=False)
            step(2, 2, 1)
            step(3, 3, 1)
            with act.Fori(1, NT // 4) as q:
                for u in range(4):
                    step(4 * q + u, u, 2 * q + u // 2)
            step(16, 0, 8, attn=False)
            step(17, 1, 8, attn=False, mid=False)

            act.wait_ge(s_o, NT)
            act.wait_ge(s_s, NT)
            for e in (6, 7):
                act.wait_ge(s_ld[1], 16 * (4 + e))
                act.activation(flat(w13_hi, e), w13_raw(), ACT.Copy).then_inc(s_lhi, 1)
                act.wait_ge(s_ld[0], 16 * (4 + e))
                act.activation(flat(w2_hi, e), w2_raw(), ACT.Copy).then_inc(s_lhi, 1)

            def estep(i, u, q, new=True, up=True, down=True):
                if new:
                    k = u % 2
                    if past(i, 2):
                        act.wait_ge(s_up, i - 1)
                    evac(s_te, i + 1, eT_hi[k][:, :, :], psXe[:, 0:D].rearrange("p (c n) -> p c n", c=DC), s_eh)
                if down:
                    k = (u - 3) % 2
                    if past(i, 5):
                        act.wait_ge(s_dn, i - 4)
                    evac(s_the, i - 2, ehT_hi[k], psHe[:, 0:H].rearrange("p (c n) -> p c n", c=DC), s_heh)
                if up:
                    act.wait_ge(s_ub, i)
                    if past(i, 3):
                        act.wait_ge(s_the, i - 2)
                    act.activation(ehid[:, (u - 1) % 2, :], u13[(u - 1) % 4][:, 0:H], ACT.Silu).then_inc(s_si, 1)

            for i in range(8):
                estep(i, i % 4, i // 4, up=i >= 1, down=i >= 3)
            with act.Fori(2, MAXT // 4) as q:
                for u in range(4):
                    estep(4 * q + u, u, q)
            for i in range(MAXT // 4 * 4, MAXT + 3):
                estep(i, i % 4, i // 4, new=i < MAXT, up=i - 1 < MAXT)

        @block.vector
        def _(v):
            for t in (encT_hi, encT_lo):
                v.memset(t.bitcast(F32)[:, :, :, KEYS:256], 0.0).then_inc(s_pad, 1)
            v.memset(probs[:, :, KEYS:256], 0.0).then_inc(s_pad, 1)

            def ln_stats(src, k, bn, mvs, n):
                v.bn_stats(st6[:, k, :], src).then_inc(bn, 1)
                v.wait_ge(bn, n)
                if not isinstance(n, int):
                    apart(v, s_pv)
                v.bn_aggr(mv[:, k, :], st6[:, k, :]).then_inc(mvs, 1)

            def ln1_stats(t, n):
                ln_stats(xt(t), 0, s_bn1, s_mv1, n)

            def ln1_apply(t, k, n):
                v.wait_ge(s_rs1, n)
                if past(n, 3):
                    v.wait_ge(s_t1, n - 2)
                v.tensor_scalar(xn[:, k, :], xt(t), mv[:, 0, 0:1], rstd[:, 0:1], ALU.subtract, ALU.mult).then_inc(s_xn, 1)

            def xt(t):
                if isinstance(t, int):
                    return x_all[:, t, :]
                return x_all[:, bass.ds(t, 1), :].rearrange("p a d -> p (a d)")

            v.wait_ge(s_x[0], 16)
            ln1_stats(0, 1)
            for n in range(NSET):
                v.wait_ge(s_shi, n + 1)
                for raw, hi, lo in setup_parts(n):
                    mm = v.tensor_tensor(lo, raw, hi.bitcast(F32), ALU.subtract)
                mm.then_inc(s_slo, 1)
                if n == 0:
                    ln1_apply(0, 0, 1)
                if n == 1:
                    for b in range(B):
                        v.wait_ge(s_ewh, b + 1)
                        v.tensor_tensor(encW_lo[:, b].rearrange("p c n -> p (c n)"), [psG, psU][b][:, :],
                                        encW_hi[:, b].rearrange("p c n -> p (c n)").bitcast(F32), ALU.subtract).then_inc(s_ewl, 1)
            v.wait_ge(s_gate, 16)
            v.tensor_copy(gate_hi[:, :, :], gate_raw[:, :, :]).then_inc(s_gh, 1)
            v.wait_ge(s_gh, 1)
            v.tensor_tensor(gate_lo[:, :, :], gate_raw[:, :, :], gate_hi[:, :, :].bitcast(F32), ALU.subtract).then_inc(s_gate, 1)
            v.wait_ge(s_mask, 16)

            def lo(ready_hi, n, out, ps, hi, ready):
                v.wait_ge(ready_hi, n)
                v.tensor_tensor(out, ps, hi.bitcast(F32), ALU.subtract).then_inc(ready, 1)

            def step(i, u, pair, attn=True, mid=True, tail=True, nxt=True):
                if mid:
                    v.wait_ge(s_o, i)
                    v.tensor_tensor(xt(i - 1), psO[:, 0:D], xt(i - 1), ALU.add).then_inc(s_x1, 1)
                    v.wait_ge(s_x1, i)
                    if not isinstance(i, int):
                        apart(v, s_pv)
                    ln_stats(xt(i - 1), 1, s_bn2, s_mv2, i)
                if attn:
                    lo(s_xh, i + 1, xT_lo[:, :, :], psX[:, 0:D].rearrange("p (c n) -> p c n", c=DC), xT_hi[:, :, :], s_xl)
                if tail:
                    lo(s_hh, i - 1, hT_lo[:, :, :], psHT[:, :].rearrange("p (c n) -> p c n", c=4), hT_hi[:, :, :], s_hl)
                if attn:
                    v.wait_ge(s_s, i + 1)
                    if past(i, 1):
                        v.wait_ge(s_ex, i)
                    v.scalar_tensor_tensor(out=smk[:], in0=mt(i), scalar=NEG, in1=psS[:, 0:KEYS], op0=ALU.mult, op1=ALU.add).then_inc(s_sm, 1)
                    v.wait_ge(s_sm, i + 1)
                    v.tensor_reduce(negmax[:], smk[:], X, ALU.max, negate=True).then_inc(s_nm, 1)
                if mid:
                    v.wait_ge(s_rs2, i)
                    if u % 2 == 1 and past(i, 5):
                        v.wait_ge(s_row, 8 * (pair - 1))
                    v.tensor_scalar(xn2[:, (u - 1) % 4, :], xt(i - 1), mv[:, 1, 0:1], rstd[:, 1:2], ALU.subtract, ALU.mult).then_inc(s_xn2, 1)
                if attn:
                    v.wait_ge(s_ex, i + 1)
                    v.reciprocal(prcp[:, u % 2:u % 2 + 1], psum_p[:, u % 2:u % 2 + 1]).then_inc(s_rc, 1)
                    v.wait_ge(s_rc, i + 1)
                    v.tensor_scalar(probs[:, u % 2, 0:KEYS], probs[:, u % 2, 0:KEYS], prcp[:, u % 2:u % 2 + 1], None, ALU.mult).then_inc(s_p, 1)
                if mid:
                    lo(s_x2h, i, x2T_lo[:, :, :], psX2[:, 0:D].rearrange("p (c n) -> p c n", c=DC), x2T_hi[:, :, :], s_x2l)
                if tail:
                    v.wait_ge(s_z, i - 1)
                    v.scalar_tensor_tensor(out=xt(i - 2), in0=psX[:, D:2 * D], scalar=0.5, in1=xt(i - 2), op0=ALU.mult, op1=ALU.add).then_inc(s_zd, 1)
                if nxt:
                    if isinstance(i, int) and i == 1:
                        v.wait_ge(s_x[1], 32)
                    ln1_stats(i + 1, i + 2)
                if mid:
                    v.wait_ge(s_gl, i)
                    v.tensor_copy(logit[:, (u - 1) % 2, :], psX2[:, D:D + NE]).then_inc(s_lg, 1)
                    v.wait_ge(s_th, i)
                    if past(i, 2):
                        v.wait_ge(s_ht, i - 1)
                    v.scalar_tensor_tensor(out=gsil[:], in0=tanh_g[:], scalar=1.0, in1=psG[:, :], op0=ALU.add, op1=ALU.mult).then_inc(s_gs, 1)
                if nxt:
                    ln1_apply(i + 1, (u + 1) % 2, i + 2)
                if attn:
                    lo(s_ph, i + 1, pT_lo[:, :, :], psPT[:, 0:256].rearrange("p (c n) -> p c n", c=2), pT_hi[:, :, :], s_pl)
                if mid:
                    if u % 2 == 0:
                        route(pair)
                    v.wait_ge(s_u, i)
                    v.wait_ge(s_gs, i)
                    v.tensor_tensor(hid[:], gsil[:], psU[:, :], ALU.mult).then_inc(s_h, 1)
                    if u % 2 == 1 and past(i, 3):
                        place(pair)

            def mt(t):
                if isinstance(t, int):
                    return mask_sb[:, t, :]
                return mask_sb[:, bass.ds(t, 1), :].rearrange("p a d -> p (a d)")

            RSTEPS = 17

            def over_e(a):
                return a.unsqueeze(2).to_broadcast([P, 2, NE])

            def route(n):
                done = [0]

                def chain(ins):
                    done[0] += 1
                    ins.then_inc(s_rt, 1)
                    v.wait_ge(s_rt, RSTEPS * (n - 1) + done[0])

                v.wait_ge(s_lg, 2 * n)
                chain(v.tensor_reduce(rmax[:], logit[:, :, :], X, ALU.max))
                v.tensor_tensor(ex[:, :, :], logit[:, :, :], over_e(rmax[:]), ALU.subtract).then_inc(s_lc, 1)
                v.wait_ge(s_re, n)
                chain(v.tensor_reduce(rsum[:], ex[:, :, :], X, ALU.add))
                chain(v.reciprocal(rrcp[:], rsum[:]))
                chain(v.tensor_tensor(score[:, :, :], ex[:, :, :], over_e(rrcp[:]), ALU.mult))
                if past(n, 2):
                    v.wait_ge(s_row, 8 * (n - 1))
                for s in range(TOP):
                    src = score if s == 0 else rest
                    chain(v.tensor_reduce(wgt[:, s, :], src[:, :, :], X, ALU.max))
                    chain(v.tensor_tensor(cand[:, :, :], src[:, :, :], over_e(wgt[:, s, :]), ALU.is_equal))
                    chain(v.tensor_tensor(cand[:, :, :], cand[:, :, :], desc[:, :, :], ALU.mult))
                    chain(v.tensor_reduce(first[:], cand[:, :, :], X, ALU.max))
                    chain(v.tensor_tensor(hot[:, s, :, :], cand[:, :, :], over_e(first[:]), ALU.is_equal))
                    if s == 0:
                        chain(v.scalar_tensor_tensor(out=rest[:, :, :], in0=hot[:, 0, :, :], scalar=-2.0, in1=score[:, :, :], op0=ALU.mult, op1=ALU.add))
                v.tensor_tensor(member[:, :, :], hot[:, 0, :, :], hot[:, 1, :, :], ALU.add).then_inc(s_mem, 1)

            def place(n):
                base = RSTEPS * (n - 1) + 15
                v.wait_ge(s_rk, n)
                v.tensor_tensor(rank[:, :, :], psPT[:, 256:272].rearrange("p (t e) -> p t e", t=2),
                                next_row[:, :].unsqueeze(1).to_broadcast([P, 2, NE]), ALU.add).then_inc(s_rt, 1)
                v.wait_ge(s_rt, base + 1)
                v.tensor_tensor(next_row[:, :], psPT[:, 272:280], next_row[:, :], ALU.add).then_inc(s_rr, 1)
                v.tensor_tensor(rsel[:, :, :, :].rearrange("p s t e -> p s (t e)"), hot[:, :, :, :].rearrange("p s t e -> p s (t e)"),
                                rank[:, :, :].rearrange("p t e -> p (t e)").unsqueeze(1).to_broadcast([P, TOP, 2 * NE]), ALU.mult).then_inc(s_rt, 1)
                v.wait_ge(s_rt, base + 2)
                if past(n, 2):
                    for k in range(4):
                        v.wait_ge(s_sc[k], 16 * (n - 1))
                with nc.allow_low_precision(reason="one row number of each sum, under 2^24, is not 0: exact"):
                    v.tensor_reduce(pos_i[:, :, :], rsel[:, :, :, :], X, ALU.add).then_inc(s_pos, 1)

            v.wait_ge(s_const, NCONST)
            step(0, 0, 0, mid=False, tail=False)
            step(1, 1, 0, tail=False)
            step(2, 2, 1)
            step(3, 3, 1)
            with v.Fori(1, NT // 4 - 1) as q:
                for u in range(4):
                    step(4 * q + u, u, 2 * q + u // 2)
            for i in range(12, NT):
                step(i, i % 4, i // 2, nxt=i + 1 < NT)
            step(16, 0, 8, attn=False, nxt=False)
            place(NT // 2)
            lo(s_hh, NT, hT_lo[:, :, :], psHT[:, :].rearrange("p (c n) -> p c n", c=4), hT_hi[:, :, :], s_hl)

            done = [0]

            def chain(ins):
                done[0] += 1
                ins.then_inc(s_tb, 1)
                v.wait_ge(s_tb, done[0])

            v.wait_ge(s_rr, NT // 2)
            chain(v.tensor_tensor(cnt[:], next_row[0:1, :], base_row[:], ALU.subtract))
            v.tensor_copy(fill_i[:], next_row[0:1, :]).then_inc(s_tab, 1)
            chain(v.tensor_tensor(over[:, :, :], cnt[:].unsqueeze(2).to_broadcast([1, NE, NT]), m128[:, :, :], ALU.is_gt))
            chain(v.tensor_reduce(ntile[:], over[:, :, :], X, ALU.add))
            chain(v.tensor_tensor(cumx[:, :, :], ntile[:].unsqueeze(1).to_broadcast([1, NE, NE]), upto[:, :, :], ALU.mult))
            chain(v.tensor_reduce(cum[:], cumx[:, :, :], X, ALU.add))
            chain(v.tensor_tensor(ended, tile_no[:, :, :], cum[:].unsqueeze(1).to_broadcast([1, MAXT, NE]), ALU.is_ge))
            chain(v.tensor_reduce(te[:], ended, X, ALU.add))
            chain(v.tensor_tensor(ended, ended, ntile[:].unsqueeze(1).to_broadcast([1, MAXT, NE]), ALU.mult))
            chain(v.tensor_reduce(tstart[:], ended, X, ALU.add))
            chain(v.tensor_tensor(trow[:], tile_no[:, :, 0], tstart[:], ALU.subtract))
            chain(v.tensor_scalar(trow2[:], te[:], float(REGION), None, ALU.mult))
            chain(v.scalar_tensor_tensor(out=trow2[:], in0=trow[:], scalar=128.0, in1=trow2[:], op0=ALU.mult, op1=ALU.add))
            v.tensor_scalar(te_i[:], te[:], float(NE - 1), None, ALU.min).then_inc(s_tab, 1)
            v.tensor_scalar(trow_i[:], trow2[:], float(FILLER), None, ALU.min).then_inc(s_tab, 1)

            v.wait_ge(s_z, NT)
            v.scalar_tensor_tensor(out=xt(NT - 1), in0=psX[:, D:2 * D], scalar=0.5, in1=xt(NT - 1), op0=ALU.mult, op1=ALU.add).then_inc(s_zd, 1)

            for e in (6, 7):
                for k, (wh, wl, raw) in enumerate(((w13_hi, w13_lo, w13_raw()), (w2_hi, w2_lo, w2_raw()))):
                    v.wait_ge(s_lhi, 2 * (e - 6) + k + 1)
                    v.tensor_tensor(flat(wl, e), raw, flat(wh, e).bitcast(F32), ALU.subtract).then_inc(s_llo, 1)
            v.wait_ge(s_bias, 16)
            v.wait_ge(s_tab, 3)

            def estep(i, u, q, new=True, up=True, down=True, dest=True):
                if dest:
                    k = (u - 2) % 4
                    if past(i, 6):
                        v.wait_ge(s_ys[k], 16 * (q - 1 if u < 2 else q))
                        if not isinstance(i, int):
                            apart(v, s_pv)
                    v.tensor_copy(dest_row[:, k:k + 1], rin[:, k, D:D + 1].bitcast(I32)).then_inc(s_ix, 1)
                if new:
                    k = u % 2
                    lo(s_eh, i + 1, eT_lo[k][:, :, :], psXe[:, 0:D].rearrange("p (c n) -> p c n", c=DC), eT_hi[k][:, :, :], s_el)
                if down:
                    k = (u - 3) % 2
                    lo(s_heh, i - 2, ehT_lo[k], psHe[:, 0:H].rearrange("p (c n) -> p c n", c=DC), ehT_hi[k], s_hel)
                if up:
                    e = v.value_load(te_i[0:1, bass.ds(i - 1, 1)], min_val=0, max_val=NE - 1)
                    v.wait_ge(s_up, i)
                    if past(i, 5):
                        v.wait_ge(s_yo, i - 4)
                    v.tensor_tensor(u13[(u - 1) % 4][:, 0:2 * H], psUe[(u - 1) % 2][:, :],
                                    bias_all[:, bass.ds(e, 1), 0:2 * H].rearrange("p a n -> p (a n)"), ALU.add).then_inc(s_ub, 1)
                if down:
                    e = v.value_load(te_i[0:1, bass.ds(i - 3, 1)], min_val=0, max_val=NE - 1)
                    v.wait_ge(s_dn, i - 2)
                    if past(i, 5):
                        v.wait_ge(s_yo, i - 4)
                    v.tensor_tensor(yb[:, (u - 3) % 2, :], psYe[(u - 3) % 2][:, 0:D],
                                    bias_all[:, bass.ds(e, 1), 2 * H:3 * H].rearrange("p a n -> p (a n)"), ALU.add).then_inc(s_yb, 1)

            for i in range(8):
                estep(i, i % 4, i // 4, up=i >= 1, down=i >= 3, dest=i >= 2)
            with v.Fori(2, MAXT // 4) as q:
                for u in range(4):
                    estep(4 * q + u, u, q)
            for i in range(MAXT // 4 * 4, MAXT + 3):
                estep(i, i % 4, i // 4, new=i < MAXT, up=i - 1 < MAXT, dest=i - 2 < MAXT)

            for c in range(4):
                v.wait_ge(s_c[c % 3], 32 if c < 3 else 64)
                v.tensor_tensor(x_all[:, 4 * c:4 * c + 4, :], x_all[:, 4 * c:4 * c + 4, :], comb(c)[:, 0], ALU.add).then_inc(s_c1, 1)
                v.wait_ge(s_c1, c + 1)
                v.tensor_tensor(x_all[:, 4 * c:4 * c + 4, :], x_all[:, 4 * c:4 * c + 4, :], comb(c)[:, 1], ALU.add).then_inc(s_c2, 1)

        @block.gpsimd
        def _(g):
            made = [0]

            def make(ins):
                made[0] += 1
                return ins.then_inc(s_const, 1)

            make(g.memset(nhalf[:], -0.5))
            make(g.memset(ident[:], 0.0))
            make(g.memset(ones[:], 1.0))
            make(g.memset(earlier[:], 0.0))
            make(g.memset(fill_blk[:], 0.0))
            make(g.memset(upto[:], 0.0))
            make(g.memset(rows[:, :, D + 1:ROW], 0.0))
            g.wait_ge(s_const, made[0])
            make(g.affine_select(out=ident[:], in_=ident[:], compare_op=ALU.not_equal, fill=1.0, base=0, pattern=[[-1, P]], channel_multiplier=1))
            make(g.affine_select(out=earlier[:], in_=earlier[:], compare_op=ALU.is_ge, fill=1.0, base=0, pattern=[[-1, P]], channel_multiplier=1))
            make(g.affine_select(out=upto[:], in_=upto[:], compare_op=ALU.is_gt, fill=1.0, base=0, pattern=[[-1, NE], [1, NE]], channel_multiplier=0))
            make(g.iota(fill_blk[:, D:D + 1].bitcast(I32), pattern=[[0, 1]], base=SKIP, channel_multiplier=1))
            make(g.iota(dest_i[:], pattern=[[S, B], [1, TB], [T, TOP]], base=0, channel_multiplier=TB))
            make(g.iota(desc[:], pattern=[[0, 2], [-1, NE]], base=NE, channel_multiplier=0, allow_small_or_imprecise_dtypes=True))
            make(g.iota(next_row[:], pattern=[[REGION, NE]], base=0, channel_multiplier=0, allow_small_or_imprecise_dtypes=True))
            make(g.iota(base_row[:], pattern=[[REGION, NE]], base=0, channel_multiplier=0, allow_small_or_imprecise_dtypes=True))
            make(g.iota(m128[:], pattern=[[0, NE], [P, NT]], base=0, channel_multiplier=0, allow_small_or_imprecise_dtypes=True))
            make(g.iota(tile_no[:, :, :], pattern=[[1, MAXT], [0, NE]], base=0, channel_multiplier=0, allow_small_or_imprecise_dtypes=True))
            assert made[0] == NCONST

            def rstd_of(k, mvs, n, ves, out):
                g.wait_ge(mvs, n)
                if not isinstance(n, int):
                    apart(g, s_pg)
                g.tensor_scalar(ve[:, k:k + 1], mv[:, k, 1:2], EPS, None, ALU.add).then_inc(ves, 1)
                g.wait_ge(ves, n)
                g.tensor_tensor(rstd[:, k:k + 1], ve[:, k:k + 1], nhalf[:], ALU.pow).then_inc(out, 1)

            def step(i, u, pair, mid=True, nxt=True):
                if mid:
                    rstd_of(1, s_mv2, i, s_ve2, s_rs2)
                if nxt:
                    rstd_of(0, s_mv1, i + 2, s_ve1, s_rs1)
                if mid and u % 2 == 0:
                    g.wait_ge(s_mem, pair)
                    for t in range(2):
                        for c in range(TOP):
                            k = 2 * t + c
                            if past(i, 4):
                                g.wait_ge(s_sc[k], 16 * (pair - 1))
                                apart(g, s_pg)
                            g.tensor_copy(rows[:, k, D:D + 1].bitcast(I32), dest(i - 2 + t, c)).then_inc(s_row, 1)
                            g.tensor_scalar(rows[:, k, 0:D], xn2[:, (u - 2 + t) % 4, :], wgt[:, c, t:t + 1], None, ALU.mult).then_inc(s_row, 1)
                if past(i, 4) and (not isinstance(i, int) or i < NT):
                    split(pair - 2, u % 2)
                if u % 2 == 1 and past(i, 3):
                    scatter(pair)

            def scatter(n):
                g.wait_ge(s_pos, n)
                g.wait_ge(s_row, 8 * n)
                if not isinstance(n, int):
                    apart(g, s_pg)
                for t in range(2):
                    for s in range(TOP):
                        k = 2 * t + s
                        g.indirect_dma_start(out=sorted_rows, out_offset=bass.IndirectOffsetOnAxis(ap=pos_i[:, s, t:t + 1], axis=0),
                                             in_=rows[:, k, :], in_offset=None).then_inc(s_sc[k], 16)

            def dest(t, c):
                if isinstance(t, int):
                    return dest_i[:, t, c:c + 1]
                return dest_i[:, bass.ds(t, 1), c:c + 1].rearrange("p a s -> p (a s)")

            def split(e, odd):
                wh, wl, raw, k = (w2_hi, w2_lo, w2_raw(), 0) if odd else (w13_hi, w13_lo, w13_raw(), 1)
                g.wait_ge(s_ld[k], 16 * (e + 4))
                g.tensor_copy(flat(wh, e), raw).then_inc(s_ehi, 1)
                g.wait_ge(s_ehi, 2 * e + 1 + odd)
                g.tensor_tensor(flat(wl, e), raw, flat(wh, e).bitcast(F32), ALU.subtract).then_inc(s_elo, 1)

            rstd_of(0, s_mv1, 1, s_ve1, s_rs1)
            for i in range(4):
                step(i, i, i // 2, mid=i >= 1)
            with g.Fori(1, NT // 4 - 1) as q:
                for u in range(4):
                    step(4 * q + u, u, 2 * q + u // 2)
            for i in range(12, NT):
                step(i, i % 4, i // 2, nxt=i + 1 < NT)
            step(16, 0, 8, nxt=False)
            scatter(NT // 2)

            def ytail(j, k, n, s):
                g.wait_ge(s_yb, n)
                if s is not None:
                    g.wait_ge(s_ys[k], s)
                g.tensor_tensor(yout[k], yb[:, k % 2, :], u13[k][:, H:2 * H], ALU.mult).then_inc(s_yo, 1)
                g.wait_ge(s_yo, n)
                apart(g, s_pg)
                g.indirect_dma_start(out=expert_out, out_offset=bass.IndirectOffsetOnAxis(ap=dest_row[:, k:k + 1], axis=0),
                                     in_=yout[k], in_offset=None, bounds_check=TOP * T - 1, oob_is_err=False).then_inc(s_ys[k], 16)

            for j in range(4):
                ytail(j, j, j + 1, None)
            with g.Fori(1, 9) as q:
                for k in range(4):
                    ytail(None, k, 4 * q + k + 1, 16 * q)
            for j in range(36, MAXT):
                ytail(j, j % 4, j + 1, 16 * (j // 4))


def kernel(x, ctx_1024, mask_BxSxS2_bk0, L0_xattn_W_attn, L0_ffn_gate_w, L0_ffn_w1, L0_ffn_b1,
           L0_ffn_w2, L0_ffn_b2, L0_ffn_w3, L0_ffn_b3, L0_ffn_sw1, L0_ffn_sw2, L0_ffn_sw3):
    import concourse.bacc as bacc
    import numpy as np
    from concourse.bass_utils import run_bass_kernel_spmd

    w_attn = np.asarray(L0_xattn_W_attn)
    laid = {
        "x": np.asarray(x),
        "enc_t": np.asarray(ctx_1024).transpose(0, 2, 1),
        "mask": np.asarray(mask_BxSxS2_bk0),
        "w_ctx": w_attn[:, :D].T,
        "w_dec": w_attn[:, D:].T,
        "gate_t": np.asarray(L0_ffn_gate_w).T,
        "sw12": np.concatenate([np.asarray(L0_ffn_sw1).T, np.asarray(L0_ffn_sw2).T], axis=1),
        "sw3": np.asarray(L0_ffn_sw3).T,
        "w13": np.concatenate([np.asarray(L0_ffn_w1).transpose(0, 2, 1), np.asarray(L0_ffn_w3).transpose(0, 2, 1)], axis=2),
        "w2": np.asarray(L0_ffn_w2).transpose(0, 2, 1),
        "bias": np.concatenate([np.asarray(L0_ffn_b1), np.asarray(L0_ffn_b3), np.asarray(L0_ffn_b2)], axis=1),
    }
    nc = bacc.Bacc("TRN2", target_bir_lowering=False, num_devices=1)
    arrays = {name: np.ascontiguousarray(a) for name, a in laid.items()}
    args = [nc.dram_tensor(name, a.shape, mybir.dt.from_np(a.dtype), kind="ExternalInput").ap() for name, a in arrays.items()]
    args.append(nc.dram_tensor("out", (B, S, D), F32, kind="ExternalOutput").ap())
    bass_xattn_moe(nc, *args)
    r = run_bass_kernel_spmd(nc, [arrays], core_ids=[0])
    return r.results[0]["out"]
```

```python
from contextlib import ExitStack

import concourse.bass as bass
from concourse import mybir

F32 = mybir.dt.float32
F32R = mybir.dt.float32r
BF16 = mybir.dt.bfloat16
I32 = mybir.dt.int32
U8 = mybir.dt.uint8
ALU = mybir.AluOpType
ACT = mybir.ActivationFunctionType
X = mybir.AxisListType.X

P = 128
B, S, D = 2, 1024, 256
KEYS = 154
T = B * S
NT = T // P
TB = NT // B
DC = D // P
NE, TOP = 8, 2
H = 256
FI = 512
REGION = T + P
FILLER = NE * REGION
ROW = D + 4
NCONST = 17
MAXT = (T * TOP + NE * (P - 1)) // P
SKIP = 1 << 20
EPS = 1e-5
NEG = -3.0e38


def bass_xattn_moe(nc, x, enc_t, mask, w_ctx, w_dec, gate_t, sw12, sw3, w13, w2, bias, out):
    ctx = ExitStack()
    with ctx:
        def sb(name, shape, dt=F32):
            return ctx.enter_context(nc.sbuf_tensor(name, shape, dt))

        def bank(name):
            return ctx.enter_context(nc.psum_tensor(name, [P, 512], F32))

        def sem(name):
            return ctx.enter_context(nc.semaphore(name))

        sorted_rows = nc.dram_tensor("sorted_rows", [FILLER + P, ROW], F32, kind="Internal").ap()
        expert_out = nc.dram_tensor("expert_out", [TOP * T, D], F32, kind="Internal").ap()

        x_all = sb("x_all", [P, NT, D])
        w13_hi = sb("w13_hi", [P, NE, DC, 2 * H], F32R)
        w13_lo = sb("w13_lo", [P, NE, DC, 2 * H], F32R)
        w2_hi = sb("w2_hi", [P, NE, DC, D], F32R)
        w2_lo = sb("w2_lo", [P, NE, DC, D], F32R)
        sw12_hi = sb("sw12_hi", [P, DC, 2 * FI], F32R)
        sw12_lo = sb("sw12_lo", [P, DC, 2 * FI], F32R)
        sw3_hi = sb("sw3_hi", [P, FI // P, D], F32R)
        sw3_lo = sb("sw3_lo", [P, FI // P, D], F32R)
        bias_all = sb("bias_all", [P, NE, 3 * H])
        stage = sb("stage", [P, 2, 1024])
        gate_raw = sb("gate_raw", [P, DC, NE])
        gate_hi = sb("gate_hi", [P, DC, NE], F32R)
        gate_lo = sb("gate_lo", [P, DC, NE], F32R)
        mask_words = sb("mask_words", [P, NT * KEYS // 4])
        mask_sb = mask_words[:, :].bitcast(U8).rearrange("p (t k) -> p t k", k=KEYS)
        def att(t, e):
            return t[:, e, :, :].rearrange("p c n -> p (c n)")
        encT_hi = att(w13_hi, 7).rearrange("p (b c k) -> p b c k", b=B, c=DC)
        encT_lo = att(w13_lo, 7).rearrange("p (b c k) -> p b c k", b=B, c=DC)
        encW_hi = att(w13_hi, 6).rearrange("p (b c n) -> p b c n", b=B, c=2)
        encW_lo = att(w13_lo, 6).rearrange("p (b c n) -> p b c n", b=B, c=2)
        wdec_hi = w2_hi[:, 7, :, :]
        wdec_lo = w2_lo[:, 7, :, :]

        ident = sb("ident", [P, P])
        earlier = sb("earlier", [P, P], BF16)
        ones = sb("ones", [P, P], BF16)
        nhalf = sb("nhalf", [P, 1])
        silu_warm = sb("silu_warm", [1, 1])
        desc = sb("desc", [P, 2, NE])
        dest_i = sb("dest_i", [P, NT, TOP], I32)
        fill_blk = sb("fill_blk", [P, ROW])
        next_row = sb("next_row", [P, NE])
        base_row = sb("base_row", [1, NE])
        m128 = sb("m128", [1, NE, NT])
        upto = sb("upto", [1, NE, NE])

        st1 = sb("st1", [P, TB, 6])
        mv1 = sb("mv1", [P, NT, 2])
        ve1 = sb("ve1", [P, NT])
        rstd1 = sb("rstd1", [P, NT])
        st2 = sb("st2", [P, 6])
        mv2 = sb("mv2", [P, 2])
        ve2 = sb("ve2", [P, 1])
        rstd2 = sb("rstd2", [P, 1])
        xn = sb("xn", [P, 2, D])
        xT_hi = sb("xT_hi", [P, DC, P], F32R)
        xT_lo = sb("xT_lo", [P, DC, P], F32R)
        smk = sb("smk", [P, KEYS])
        negmax = sb("negmax", [P, 1])
        probs = sb("probs", [P, 2, D])
        psum_p = sb("psum_p", [P, 2])
        prcp = sb("prcp", [P, 2])
        pT_hi = sb("pT_hi", [P, 2, P], F32R)
        pT_lo = sb("pT_lo", [P, 2, P], F32R)
        xn2 = sb("xn2", [P, 4, D])
        x2T_hi = sb("x2T_hi", [P, DC, P], F32R)
        x2T_lo = sb("x2T_lo", [P, DC, P], F32R)
        tanh_g = sb("tanh_g", [P, FI])
        gsil = sb("gsil", [P, FI])
        hid = sb("hid", [P, FI])
        hT_hi = sb("hT_hi", [P, 4, P], F32R)
        hT_lo = sb("hT_lo", [P, 4, P], F32R)
        logit = sb("logit", [P, 2, NE])
        rmax = sb("rmax", [P, 2])
        ex = sb("ex", [P, 2, NE])
        rsum = sb("rsum", [P, 2])
        rrcp = sb("rrcp", [P, 2])
        score = sb("score", [P, 2, NE])
        cand = sb("cand", [P, 2, NE])
        first = sb("first", [P, 2])
        hot = sb("hot", [P, TOP, 2, NE])
        wgt = sb("wgt", [P, TOP, 2])
        rest = sb("rest", [P, 2, NE])
        member = sb("member", [P, 2, NE], BF16)
        rank = sb("rank", [P, 2, NE])
        rsel = sb("rsel", [P, TOP, 2, NE])
        pos_i = sb("pos_i", [P, TOP, 2], I32)
        rows = sb("rows", [P, 4, ROW])
        cnt = sb("cnt", [1, NE])
        over = sb("over", [1, NE, NT])
        ntile = sb("ntile", [1, NE])
        cumx = sb("cumx", [1, NE, NE])
        cum = sb("cum", [1, NE])
        te = sb("te", [1, MAXT])
        tstart = sb("tstart", [1, MAXT])
        trow = sb("trow", [1, MAXT])
        trow2 = sb("trow2", [1, MAXT])
        te_i = sb("te_i", [1, MAXT], I32)
        trow_i = sb("trow_i", [1, MAXT], I32)
        fill_i = sb("fill_i", [1, NE], I32)
        tile_no = sb("tile_no", [1, MAXT, NE])
        ended = gsil[0:1, 0:MAXT * NE].rearrange("p (j e) -> p j e", e=NE)
        rin = rows
        eT_hi = [x2T_hi[:, :, :], xT_hi[:, :, :]]
        eT_lo = [x2T_lo[:, :, :], xT_lo[:, :, :]]
        ehT_hi = [pT_hi[:, :, :], hT_hi[:, 0:2, :]]
        ehT_lo = [pT_lo[:, :, :], hT_lo[:, 0:2, :]]
        u13 = [tanh_g[:, :], gsil[:, :], hid[:, :], stage[:, 0, 0:512]]
        dest_row = sb("dest_row", [P, 4], I32)
        ehid = xn
        yb = probs
        yout = [xn2[:, 0, :], xn2[:, 1, :], stage[:, 1, 0:256], stage[:, 1, 256:512]]

        psX = bank("psX")
        psX2 = bank("psX2")
        psPT = bank("psPT")
        psHT = bank("psHT")
        psS = bank("psS")
        psG = bank("psG")
        psU = bank("psU")
        psO = bank("psO")
        psXe, psHe = psX2, psHT
        psUe = [psG, psU]
        psYe = [psO, psS]

        s_const = sem("constants_made")
        s_gh = sem("gate_hi")
        s_x = [sem("x_pair0"), sem("x_batch0"), sem("x_batch1")]
        s_mask = sem("mask_loaded")
        s_gate = sem("gate_loaded")
        s_bias = sem("bias_loaded")
        s_ld = [sem("stage0_loaded"), sem("stage1_loaded")]
        s_shi = sem("setup_hi")
        s_slo = sem("setup_lo")
        s_pad = sem("enc_padded")
        s_ehi = sem("expert_w_hi")
        s_elo = sem("expert_w_lo")
        s_w7 = sem("expert7_loaded")
        s_lhi = sem("late_w_hi")
        s_llo = sem("late_w_lo")
        s_ew = sem("encW_product")
        s_ewh = sem("encW_hi")
        s_ewl = sem("encW_lo")
        s_bn1, s_mv1, s_ve1, s_rs1, s_xn = sem("ln1_stats"), sem("ln1_mv"), sem("ln1_ve"), sem("ln1_rstd"), sem("xn_ready")
        s_bn2, s_mv2, s_ve2, s_rs2, s_xn2 = sem("ln2_stats"), sem("ln2_mv"), sem("ln2_ve"), sem("ln2_rstd"), sem("xn2_ready")
        s_t1, s_xh, s_xl = sem("xT_psum"), sem("xT_hi_ready"), sem("xT_lo_ready")
        s_s, s_sm, s_nm, s_ex, s_rc, s_p = sem("scores"), sem("scores_masked"), sem("negmax_ready"), sem("exp_done"), sem("prcp_ready"), sem("probs_ready")
        s_tp, s_ph, s_pl = sem("pT_psum"), sem("pT_hi_ready"), sem("pT_lo_ready")
        s_o, s_x1 = sem("attn_out"), sem("x1_ready")
        s_t2, s_x2h, s_x2l = sem("x2T_psum"), sem("x2T_hi_ready"), sem("x2T_lo_ready")
        s_gl, s_lg = sem("gate_logits"), sem("logits_copied")
        s_g, s_th, s_gs = sem("ffn_g"), sem("tanh_done"), sem("gsil_ready")
        s_u, s_h = sem("ffn_u"), sem("hidden_ready")
        s_ht, s_hh, s_hl = sem("hT_psum"), sem("hT_hi_ready"), sem("hT_lo_ready")
        s_z, s_zd = sem("ffn_z"), sem("z_added")
        s_rt = sem("route_step")
        s_lc = sem("route_shifted")
        s_re = sem("route_exp")
        s_mem = sem("members_ready")
        s_rk = sem("ranks")
        s_rr = sem("ranks_read")
        s_wr = sem("weights_ready")
        s_pos = sem("pos_ready")
        s_row = sem("rows_scaled")
        s_dst = sem("row_destinations")
        s_sc = [sem(f"rows_scattered{k}") for k in range(4)]
        s_tb = sem("table_step")
        s_tab = sem("table_ready")
        s_fill = sem("filler_written")
        s_rin = [sem(f"rin{k}_loaded") for k in range(4)]
        s_te, s_eh, s_el = sem("eT_psum"), sem("eT_hi_ready"), sem("eT_lo_ready")
        s_up, s_ub, s_si = sem("e_up"), sem("e_biased"), sem("e_silu")
        s_the, s_heh, s_hel = sem("ehT_psum"), sem("ehT_hi_ready"), sem("ehT_lo_ready")
        s_ix = sem("dest_rows_copied")
        s_dn, s_yb, s_yo = sem("e_down"), sem("e_y_biased"), sem("e_y_ready")
        s_ys = [sem(f"y_scattered{k}") for k in range(4)]
        s_c = [sem(f"comb{k}_loaded") for k in range(3)]
        s_c1, s_c2 = sem("comb_first"), sem("comb_done")
        s_out = sem("out_stored")

        s_pv, s_pp, s_pg = sem("passed_dve"), sem("passed_pe"), sem("passed_pool")

        block = ctx.enter_context(nc.Block())

        def apart(engine, passed):
            engine.sem_inc(passed, 1)

        def fill(engine, experts):
            engine.wait_ge(s_tab, 1)
            for e in experts:
                r = engine.value_load(fill_i[0:1, e:e + 1], min_val=e * REGION, max_val=e * REGION + T)
                engine.dma_start(sorted_rows[bass.ds(r, P), :], fill_blk[:]).then_inc(s_fill, 16)

        def expert_of(engine, seen, i, u, before):
            key = (i if isinstance(i, int) else u) - before
            if key not in seen:
                seen[key] = engine.value_load(te_i[0:1, bass.ds(i - before, 1)], min_val=0, max_val=NE - 1)
            return seen[key]

        def past(i, n):
            return not isinstance(i, int) or i >= n

        NSET = 5
        wctx_hi = hT_hi[:, :, :].rearrange("p a b -> p (a b)").rearrange("p (c n) -> p c n", c=DC)
        wctx_lo = hT_lo[:, :, :].rearrange("p a b -> p (a b)").rearrange("p (c n) -> p c n", c=DC)

        def setup_parts(n):
            raw = stage[:, n % 2, :]
            if n == 0:
                r = raw[:, 0:B * DC * KEYS].rearrange("p (b c k) -> p b c k", b=B, c=DC)
                return [(r[:, b], encT_hi[:, b, :, 0:KEYS], encT_lo[:, b, :, 0:KEYS]) for b in range(B)]
            if n == 1:
                return [(raw[:, 0:512].rearrange("p (c n) -> p c n", c=DC), wctx_hi, wctx_lo),
                        (raw[:, 512:1024].rearrange("p (c n) -> p c n", c=DC), wdec_hi, wdec_lo)]
            if n < 4:
                return [(raw, sw12_hi[:, n - 2, :], sw12_lo[:, n - 2, :])]
            return [(raw, sw3_hi[:, :, :].rearrange("p c n -> p (c n)"), sw3_lo[:, :, :].rearrange("p c n -> p (c n)"))]

        def w13_raw():
            return stage[:, 1, :]

        def w2_raw():
            return stage[:, 0, 0:DC * D]

        def flat(t, e):
            return t[:, bass.ds(e, 1), :, :].rearrange("p a c n -> p (a c n)")

        def comb(c):
            return bias_all[:, :, :].rearrange("p e n -> p (e n)").rearrange("p (k s t d) -> p k s t d", k=3, s=TOP, t=4)[:, c % 3]

        w13_raw7 = [xn[:, :, :].rearrange("p a d -> p (a d)"), probs[:, :, :].rearrange("p a d -> p (a d)")]
        w2_raw7 = mask_words[:, 0:DC * D]

        @block.sync
        def _(sp):
            xv = x.rearrange("b (p t) d -> p b t d", t=TB)
            sp.dma_start(x_all[:, 0:2, :], xv[:, 0, 0:2, :]).then_inc(s_x[0], 16)
            sp.dma_start(stage[:, 0, 0:B * DC * KEYS].rearrange("p (b c k) -> p b c k", b=B, c=DC),
                         enc_t.rearrange("b (c p) k -> p b c k", p=P)).then_inc(s_ld[0], 16)
            sp.dma_start(stage[:, 1, :].rearrange("p (w c n) -> p w c n", w=2, c=DC)[:, 0], w_ctx.rearrange("(c p) n -> p c n", p=P)).then_inc(s_ld[1], 16)
            sp.dma_start(stage[:, 1, :].rearrange("p (w c n) -> p w c n", w=2, c=DC)[:, 1], w_dec.rearrange("(c p) n -> p c n", p=P)).then_inc(s_ld[1], 16)
            for c in range(DC):
                sp.wait_ge(s_slo, c + 1)
                sp.dma_start(stage[:, c, :], sw12[c * P:(c + 1) * P, :]).then_inc(s_ld[c], 16)
            sp.wait_ge(s_slo, 3)
            sp.dma_start(stage[:, 0, :].rearrange("p (c n) -> p c n", n=D), sw3.rearrange("(c p) n -> p c n", p=P)).then_inc(s_ld[0], 16)

            def load_w13(e):
                sp.dma_start(w13_raw().rearrange("p (c n) -> p c n", c=DC), w13.rearrange("e (c p) n -> p e c n", p=P)[:, bass.ds(e, 1)].rearrange("p a c n -> p (a c) n")).then_inc(s_ld[1], 16)

            def load_w2(e):
                sp.dma_start(w2_raw().rearrange("p (c n) -> p c n", c=DC), w2.rearrange("e (c p) n -> p e c n", p=P)[:, bass.ds(e, 1)].rearrange("p a c n -> p (a c) n")).then_inc(s_ld[0], 16)

            sp.wait_ge(s_slo, 4)
            load_w13(0)
            sp.wait_ge(s_slo, 5)
            load_w2(0)
            with sp.Fori(1, 6) as e:
                sp.wait_ge(s_elo, 2 * e - 1)
                load_w13(e)
                sp.wait_ge(s_elo, 2 * e)
                load_w2(e)
            sp.dma_start(bias_all[:, :, :].rearrange("p e n -> p (e n)"), bias.rearrange("e n -> (e n)").partition_broadcast(P)).then_inc(s_bias, 16)
            sp.wait_ge(s_elo, 11)
            load_w13(6)
            sp.wait_ge(s_elo, 12)
            load_w2(6)
            sp.dma_start(sorted_rows[FILLER:FILLER + P, :], fill_blk[:]).then_inc(s_fill, 16)
            sp.wait_ge(s_tp, NT)
            for c in range(DC):
                sp.dma_start(w13_raw7[c], w13[7, c * P:(c + 1) * P, :]).then_inc(s_w7, 16)
            sp.dma_start(w2_raw7.rearrange("p (c n) -> p c n", c=DC), w2[7].rearrange("(c p) n -> p c n", p=P)).then_inc(s_w7, 16)
            fill(sp, range(0, NE // 2))
            sp.wait_ge(s_fill, 16 * (NE + 1))
            sp.wait_ge(s_tab, 3)
            for k in range(4):
                sp.wait_ge(s_sc[k], 16 * NT // 2)

            def load_rows(j, k, reuse):
                if reuse is not None:
                    sp.wait_ge(s_ix, reuse)
                r = sp.value_load(trow_i[0:1, bass.ds(j, 1)], min_val=0, max_val=FILLER)
                sp.dma_start(rin[:, k, :], sorted_rows[bass.ds(r, P), :]).then_inc(s_rin[k], 16)

            for j in range(4):
                load_rows(j, j, None)
            with sp.Fori(1, 9) as q:
                for k in range(4):
                    load_rows(4 * q + k, k, 4 * q + k - 3)
            for j in range(36, MAXT):
                load_rows(j, j % 4, j - 3)

            for k in range(4):
                sp.wait_ge(s_ys[k], 16 * len(range(k, MAXT, 4)))
            yv = expert_out.rearrange("(s b p t) d -> p s b t d", s=TOP, b=B, t=TB)
            ov = out.rearrange("b (p t) d -> p b t d", t=TB)

            def load_comb(c):
                for s in range(TOP):
                    sp.dma_start(comb(c)[:, s], yv[:, s, c // 2, (c % 2) * 4:(c % 2) * 4 + 4, :]).then_inc(s_c[c % 3], 16)

            sp.wait_ge(s_yb, MAXT)
            for c in range(3):
                load_comb(c)
            sp.wait_ge(s_c2, 1)
            load_comb(3)
            for c in range(4):
                sp.wait_ge(s_c2, c + 1)
                sp.dma_start(ov[:, c // 2, (c % 2) * 4:(c % 2) * 4 + 4, :], x_all[:, 4 * c:4 * c + 4, :]).then_inc(s_out, 16)
            sp.wait_ge(s_out, 64)

        @block.tensor
        def _(pe):
            def three(o, lh, ll, rh, rl, start, stop):
                pe.matmul(o, lh, rh, start=start, stop=False)
                pe.matmul(o, lh, rl, start=False, stop=False)
                return pe.matmul(o, ll, rh, start=False, stop=stop)

            pe.wait_ge(s_slo, 2)
            pe.wait_ge(s_pad, 2)
            for b in range(B):
                for k in range(2):
                    o = [psG, psU][b][:, k * D:(k + 1) * D]
                    for c in range(DC):
                        ks = slice(k * P, (k + 1) * P)
                        mm = three(o, encT_hi[:, b, c, ks], encT_lo[:, b, c, ks], wctx_hi[:, c], wctx_lo[:, c], c == 0, c == DC - 1)
                mm.then_inc(s_ew, 1)
            pe.wait_ge(s_const, NCONST)
            pe.wait_ge(s_pad, 3)
            pe.wait_ge(s_ewl, 2)

            def step(i, u, pair, b, attn=True, mid=True, tail=True):
                late = past(i, 2)
                if attn:
                    pe.wait_ge(s_xn, i + 1)
                    if past(i, 3):
                        pe.wait_ge(s_zd, i - 2)
                    for c in range(DC):
                        mm = pe.transpose(psX[:, c * P:(c + 1) * P], xn[:, u % 2, c * P:(c + 1) * P], ident[:])
                    mm.then_inc(s_t1, 1)
                if tail:
                    pe.wait_ge(s_h, i - 1)
                    for c in range(4):
                        mm = pe.transpose(psHT[:, c * P:(c + 1) * P], hid[:, c * P:(c + 1) * P], ident[:])
                    mm.then_inc(s_ht, 1)
                if attn:
                    pe.wait_ge(s_xl, i + 1)
                    if past(i, 1):
                        pe.wait_ge(s_sm, i)
                    for c in range(DC):
                        mm = three(psS[:, 0:KEYS], xT_hi[:, c], xT_lo[:, c], encT_hi[:, b, c, 0:KEYS], encT_lo[:, b, c, 0:KEYS], c == 0, c == DC - 1)
                    mm.then_inc(s_s, 1)
                if tail:
                    pe.wait_ge(s_hl, i - 1)
                    for c in range(4):
                        mm = three(psX[:, D:2 * D], hT_hi[:, c], hT_lo[:, c], sw3_hi[:, c], sw3_lo[:, c], c == 0, c == 3)
                    mm.then_inc(s_z, 1)
                if mid:
                    pe.wait_ge(s_xn2, i)
                    if late:
                        pe.wait_ge(s_lg, i - 1)
                    for c in range(DC):
                        mm = pe.transpose(psX2[:, c * P:(c + 1) * P], xn2[:, (u - 1) % 4, c * P:(c + 1) * P], ident[:])
                    mm.then_inc(s_t2, 1)
                if attn:
                    if past(i, 1):
                        pe.wait_ge(s_x1, i)
                    for c in range(DC):
                        three(psO[:, 0:D], xT_hi[:, c], xT_lo[:, c], wdec_hi[:, c], wdec_lo[:, c], c == 0, False)
                if mid:
                    pe.wait_ge(s_x2l, i)
                    for c in range(DC):
                        mm = three(psX2[:, D:D + NE], x2T_hi[:, c], x2T_lo[:, c], gate_hi[:, c], gate_lo[:, c], c == 0, c == DC - 1)
                    mm.then_inc(s_gl, 1)
                    if late:
                        pe.wait_ge(s_gs, i - 1)
                    for c in range(DC):
                        mm = three(psG[:, :], x2T_hi[:, c], x2T_lo[:, c], sw12_hi[:, c, 0:FI], sw12_lo[:, c, 0:FI], c == 0, c == DC - 1)
                    mm.then_inc(s_g, 1)
                if attn:
                    pe.wait_ge(s_p, i + 1)
                    if u % 2 == 0 and past(i, 4):
                        pe.wait_ge(s_rr, pair - 1)
                    for c in range(2):
                        mm = pe.transpose(psPT[:, c * P:(c + 1) * P], probs[:, u % 2, c * P:(c + 1) * P], ident[:])
                    mm.then_inc(s_tp, 1)
                if mid:
                    if late:
                        pe.wait_ge(s_h, i - 1)
                    for c in range(DC):
                        mm = three(psU[:, :], x2T_hi[:, c], x2T_lo[:, c], sw12_hi[:, c, FI:2 * FI], sw12_lo[:, c, FI:2 * FI], c == 0, c == DC - 1)
                    mm.then_inc(s_u, 1)
                if attn:
                    pe.wait_ge(s_pl, i + 1)
                    if u % 2 == 1 and past(i, 3):
                        ranks(pair)
                if attn:
                    for c in range(2):
                        mm = three(psO[:, 0:D], pT_hi[:, c], pT_lo[:, c], encW_hi[:, b, c], encW_lo[:, b, c], False, c == 1)
                    mm.then_inc(s_o, 1)

            def ranks(n):
                pe.wait_ge(s_mem, n)
                m0, m1 = member[:, 0, :], member[:, 1, :]
                pe.matmul(psPT[:, 256:264], earlier[:], m0, start=True, stop=True)
                pe.matmul(psPT[:, 264:272], earlier[:], m1, start=True, stop=False)
                pe.matmul(psPT[:, 264:272], ones[:], m0, start=False, stop=True)
                pe.matmul(psPT[:, 272:280], ones[:], m0, start=True, stop=False)
                pe.matmul(psPT[:, 272:280], ones[:], m1, start=False, stop=True).then_inc(s_rk, 1)

            step(0, 0, 0, 0, mid=False, tail=False)
            pe.wait_ge(s_slo, 5)
            pe.wait_ge(s_gate, 17)
            step(1, 1, 0, 0, tail=False)
            for i in range(2, TB):
                step(i, i % 4, i // 2, 0)
            with pe.Fori(TB // 4, NT // 4) as q:
                for u in range(4):
                    step(4 * q + u, u, 2 * q + u // 2, 1)
            step(16, 0, 8, 1, attn=False)
            ranks(NT // 2)
            step(17, 1, 8, 1, attn=False, mid=False)

            pe.wait_ge(s_tab, 3)

            def estep(seen, i, u, q, new=True, up=True, down=True):
                if new:
                    k = u % 4
                    pe.wait_ge(s_rin[k], 16 * (q + 1))
                    if past(i, 1):
                        pe.wait_ge(s_el, i)
                    for c in range(DC):
                        mm = pe.transpose(psXe[:, c * P:(c + 1) * P], rin[:, k, c * P:(c + 1) * P], ident[:])
                    mm.then_inc(s_te, 1)
                elif up:
                    pe.wait_ge(s_el, i)
                if down:
                    pe.wait_ge(s_si, i - 2)
                    for c in range(DC):
                        mm = pe.transpose(psHe[:, c * P:(c + 1) * P], ehid[:, (u - 3) % 2, c * P:(c + 1) * P], ident[:])
                    mm.then_inc(s_the, 1)
                if up:
                    if isinstance(i, int) and i == 1:
                        pe.wait_ge(s_llo, 5)
                        pe.wait_ge(s_h, NT)
                        apart(pe, s_pp)
                    k = (u - 1) % 2
                    e = expert_of(pe, seen, i, u, 1)
                    wh = w13_hi[:, bass.ds(e, 1)].rearrange("p a c n -> p (a c) n")
                    wl = w13_lo[:, bass.ds(e, 1)].rearrange("p a c n -> p (a c) n")
                    for c in range(DC):
                        mm = three(psUe[k][:, :], eT_hi[k][:, c], eT_lo[k][:, c], wh[:, c], wl[:, c], c == 0, c == DC - 1)
                    mm.then_inc(s_up, 1)
                if down:
                    k = (u - 3) % 2
                    e = expert_of(pe, seen, i, u, 3)
                    wh = w2_hi[:, bass.ds(e, 1)].rearrange("p a c n -> p (a c) n")
                    wl = w2_lo[:, bass.ds(e, 1)].rearrange("p a c n -> p (a c) n")
                    pe.wait_ge(s_hel, i - 2)
                    for c in range(DC):
                        mm = three(psYe[k][:, 0:D], ehT_hi[k][:, c], ehT_lo[k][:, c], wh[:, c], wl[:, c], c == 0, c == DC - 1)
                    mm.then_inc(s_dn, 1)

            seen = {}
            for i in range(8):
                estep(seen, i, i % 4, i // 4, up=i >= 1, down=i >= 3)
            with pe.Fori(2, MAXT // 4) as q:
                seen = {}
                for u in range(4):
                    estep(seen, 4 * q + u, u, q)
            seen = {}
            for i in range(MAXT // 4 * 4, MAXT + 3):
                estep(seen, i, i % 4, i // 4, new=i < MAXT, up=i - 1 < MAXT)

        @block.scalar
        def _(act):
            xv = x.rearrange("b (p t) d -> p b t d", t=TB)
            act.dma_start(gate_raw[:], gate_t.rearrange("(c p) e -> p c e", p=P)).then_inc(s_gate, 16)
            act.dma_start(mask_sb[:, :, :].rearrange("p (b t) k -> p b (t k)", b=B), mask.rearrange("b (p t) k -> p b (t k)", t=TB)).then_inc(s_mask, 16)
            act.dma_start(x_all[:, 2:TB, :], xv[:, 0, 2:TB, :]).then_inc(s_x[1], 16)
            act.dma_start(x_all[:, TB:NT, :], xv[:, 1]).then_inc(s_x[2], 16)
            for n in range(NSET):
                act.wait_ge(s_ld[n % 2], [16, 32, 32, 48, 48][n])
                for raw, hi, _ in setup_parts(n):
                    mm = act.activation(hi, raw, ACT.Copy)
                mm.then_inc(s_shi, 1)
                if n == 1:
                    for b in range(B):
                        act.wait_ge(s_ew, b + 1)
                        act.activation(encW_hi[:, b].rearrange("p c n -> p (c n)"), [psG, psU][b][:, :], ACT.Copy).then_inc(s_ewh, 1)

            def evac(done, t, out, ps, ready):
                act.wait_ge(done, t)
                act.activation(out, ps, ACT.Copy).then_inc(ready, 1)

            def step(i, u, pair, attn=True, mid=True, tail=True):
                if attn:
                    evac(s_t1, i + 1, xT_hi[:, :, :], psX[:, 0:D].rearrange("p (c n) -> p c n", c=DC), s_xh)
                if tail:
                    evac(s_ht, i - 1, hT_hi[:, :, :], psHT[:, :].rearrange("p (c n) -> p c n", c=4), s_hh)
                if attn:
                    act.wait_ge(s_nm, i + 1)
                    if past(i, 2):
                        act.wait_ge(s_tp, i - 1)
                    act.activation(probs[:, u % 2, 0:KEYS], smk[:], ACT.Exp, bias=negmax[:, 0:1],
                                   accum_out=psum_p[:, u % 2:u % 2 + 1]).then_inc(s_ex, 1)
                if mid:
                    evac(s_t2, i, x2T_hi[:, :, :], psX2[:, 0:D].rearrange("p (c n) -> p c n", c=DC), s_x2h)
                    act.wait_ge(s_g, i)
                    if past(i, 2):
                        act.wait_ge(s_gs, i - 1)
                    act.activation(tanh_g[:], psG[:, :], ACT.Tanh, scale=0.5).then_inc(s_th, 1)
                if mid and u % 2 == 0:
                    act.wait_ge(s_lc, pair)
                    act.activation(ex[:, :, :], ex[:, :, :], ACT.Exp).then_inc(s_re, 1)
                if attn:
                    evac(s_tp, i + 1, pT_hi[:, :, :], psPT[:, 0:256].rearrange("p (c n) -> p c n", c=2), s_ph)
                if mid and u % 2 == 0:
                    if not isinstance(i, int) or i < NT - 2:
                        split_hi(pair - 1)
                if u % 2 == 1 and past(i, 3):
                    scale(pair, (u - 3) % 4)

            def split_hi(e):
                for k, (wh, raw) in ((1, (w13_hi, w13_raw())), (0, (w2_hi, w2_raw()))):
                    act.wait_ge(s_ld[k], 16 * (e + 4))
                    act.activation(flat(wh, e), raw, ACT.Copy).then_inc(s_ehi, 1)

            def scale(n, slot):
                act.wait_ge(s_mem, n)
                for t in range(2):
                    for c in range(TOP):
                        k = 2 * t + c
                        if past(n, 2):
                            act.wait_ge(s_sc[k], 16 * (n - 1))
                        act.activation(rows[:, k, 0:D], xn2[:, slot + t, :], ACT.Copy, scale=wgt[:, c, t:t + 1]).then_inc(s_row, 1)

            step(0, 0, 0, mid=False, tail=False)
            step(1, 1, 0, tail=False)
            step(2, 2, 1)
            step(3, 3, 1)
            with act.Fori(1, NT // 4 - 1) as q:
                for u in range(4):
                    step(4 * q + u, u, 2 * q + u // 2)
            for i in range(12, NT):
                step(i, i % 4, i // 2)
            step(16, 0, 8, attn=False)
            scale(NT // 2, 2)
            act.wait_ge(s_o, NT)
            act.wait_ge(s_ld[1], 16 * 10)
            act.activation(flat(w13_hi, 6), w13_raw(), ACT.Copy).then_inc(s_lhi, 1)
            act.wait_ge(s_ld[0], 16 * 10)
            act.activation(flat(w2_hi, 6), w2_raw(), ACT.Copy).then_inc(s_lhi, 1)
            fill(act, range(NE // 2, NE))
            evac(s_ht, NT, hT_hi[:, :, :], psHT[:, :].rearrange("p (c n) -> p c n", c=4), s_hh)
            act.wait_ge(s_w7, 48)
            for c in range(DC):
                act.activation(w13_hi[:, 7, c, :], w13_raw7[c], ACT.Copy).then_inc(s_lhi, 1)
            act.activation(flat(w2_hi, 7), w2_raw7, ACT.Copy).then_inc(s_lhi, 1)
            act.activation(silu_warm[:], nhalf[0:1, :], ACT.Silu)

            def estep(i, u, q, new=True, up=True, down=True):
                if new:
                    k = u % 2
                    evac(s_te, i + 1, eT_hi[k][:, :, :], psXe[:, 0:D].rearrange("p (c n) -> p c n", c=DC), s_eh)
                if down:
                    k = (u - 3) % 2
                    evac(s_the, i - 2, ehT_hi[k], psHe[:, 0:H].rearrange("p (c n) -> p c n", c=DC), s_heh)
                if up:
                    act.wait_ge(s_ub, i)
                    act.activation(ehid[:, (u - 1) % 2, :], u13[(u - 1) % 4][:, 0:H], ACT.Silu).then_inc(s_si, 1)

            for i in range(8):
                estep(i, i % 4, i // 4, up=i >= 1, down=i >= 3)
            with act.Fori(2, MAXT // 4) as q:
                for u in range(4):
                    estep(4 * q + u, u, q)
            for i in range(MAXT // 4 * 4, MAXT + 3):
                estep(i, i % 4, i // 4, new=i < MAXT, up=i - 1 < MAXT)

        @block.vector
        def _(v):
            for t in (encT_hi, encT_lo):
                v.memset(t.bitcast(F32)[:, :, :, KEYS:256], 0.0).then_inc(s_pad, 1)
            v.memset(probs[:, :, KEYS:256], 0.0).then_inc(s_pad, 1)

            def ln1_stats(a, b):
                for t in range(a, b):
                    v.bn_stats(st1[:, t % TB, :], x_all[:, t, :]).then_inc(s_bn1, 1)
                v.wait_ge(s_bn1, b)
                for t in range(a, b):
                    v.bn_aggr(mv1[:, t, :], st1[:, t % TB, :]).then_inc(s_mv1, 1)

            def ln1_apply(t, k):
                if past(t, 2):
                    v.wait_ge(s_t1, t - 1)
                m, r = ((mv1[:, t, 0:1], rstd1[:, t:t + 1]) if isinstance(t, int) else
                        (mv1[:, bass.ds(t, 1), 0:1].rearrange("p a b -> p (a b)"), rstd1[:, bass.ds(t, 1)]))
                v.tensor_scalar(xn[:, k, :], xt(t), m, r, ALU.subtract, ALU.mult).then_inc(s_xn, 1)

            def xt(t):
                if isinstance(t, int):
                    return x_all[:, t, :]
                return x_all[:, bass.ds(t, 1), :].rearrange("p a d -> p (a d)")

            v.wait_ge(s_x[0], 16)
            ln1_stats(0, 2)
            for n in range(NSET):
                v.wait_ge(s_shi, n + 1)
                for raw, hi, lo in setup_parts(n):
                    mm = v.tensor_tensor(lo, raw, hi.bitcast(F32), ALU.subtract)
                mm.then_inc(s_slo, 1)
                if n == 0:
                    v.wait_ge(s_rs1, 1)
                    ln1_apply(0, 0)
                if n == 1:
                    for b in range(B):
                        v.wait_ge(s_ewh, b + 1)
                        v.tensor_tensor(encW_lo[:, b].rearrange("p c n -> p (c n)"), [psG, psU][b][:, :],
                                        encW_hi[:, b].rearrange("p c n -> p (c n)").bitcast(F32), ALU.subtract).then_inc(s_ewl, 1)
                    v.wait_ge(s_x[1], 16)
                    ln1_stats(2, TB)
            v.wait_ge(s_gate, 16)
            v.tensor_copy(gate_hi[:, :, :], gate_raw[:, :, :]).then_inc(s_gh, 1)
            v.wait_ge(s_gh, 1)
            v.tensor_tensor(gate_lo[:, :, :], gate_raw[:, :, :], gate_hi[:, :, :].bitcast(F32), ALU.subtract).then_inc(s_gate, 1)
            v.wait_ge(s_mask, 16)

            def lo(ready_hi, n, out, ps, hi, ready):
                v.wait_ge(ready_hi, n)
                v.tensor_tensor(out, ps, hi.bitcast(F32), ALU.subtract).then_inc(ready, 1)

            def step(i, u, pair, attn=True, mid=True, tail=True, nxt=True):
                odd = u % 2 == 1 and mid and past(i, 3)
                even = u % 2 == 0 and mid
                if mid:
                    v.wait_ge(s_o, i)
                    v.tensor_tensor(xt(i - 1), psO[:, 0:D], xt(i - 1), ALU.add).then_inc(s_x1, 1)
                    if odd:
                        route(pair, 4)
                    v.wait_ge(s_x1, i)
                    if not isinstance(i, int):
                        apart(v, s_pv)
                    v.bn_stats(st2[:], xt(i - 1)).then_inc(s_bn2, 1)
                    if odd:
                        route(pair, 5)
                if attn:
                    lo(s_xh, i + 1, xT_lo[:, :, :], psX[:, 0:D].rearrange("p (c n) -> p c n", c=DC), xT_hi[:, :, :], s_xl)
                if mid:
                    v.wait_ge(s_bn2, i)
                    if not isinstance(i, int):
                        apart(v, s_pv)
                    v.bn_aggr(mv2[:], st2[:]).then_inc(s_mv2, 1)
                if odd:
                    route(pair, 6)
                if tail:
                    lo(s_hh, i - 1, hT_lo[:, :, :], psHT[:, :].rearrange("p (c n) -> p c n", c=4), hT_hi[:, :, :], s_hl)
                if odd:
                    route(pair, 7)
                if attn:
                    v.wait_ge(s_s, i + 1)
                    if past(i, 1):
                        v.wait_ge(s_ex, i)
                    v.scalar_tensor_tensor(out=smk[:], in0=mt(i), scalar=NEG, in1=psS[:, 0:KEYS], op0=ALU.mult, op1=ALU.add).then_inc(s_sm, 1)
                    if odd:
                        route(pair, 8)
                    v.wait_ge(s_sm, i + 1)
                    v.tensor_reduce(negmax[:], smk[:], X, ALU.max, negate=True).then_inc(s_nm, 1)
                if odd:
                    route(pair, 9)
                if mid:
                    v.wait_ge(s_rs2, i)
                    if u % 2 == 1 and past(i, 5):
                        v.wait_ge(s_row, 4 * (pair - 1))
                    v.tensor_scalar(xn2[:, (u - 1) % 4, :], xt(i - 1), mv2[:, 0:1], rstd2[:, 0:1], ALU.subtract, ALU.mult).then_inc(s_xn2, 1)
                if odd:
                    route(pair, 10)
                if attn:
                    v.wait_ge(s_ex, i + 1)
                    v.reciprocal(prcp[:, u % 2:u % 2 + 1], psum_p[:, u % 2:u % 2 + 1]).then_inc(s_rc, 1)
                    if odd:
                        route(pair, 11)
                    v.wait_ge(s_rc, i + 1)
                    v.tensor_scalar(probs[:, u % 2, 0:KEYS], probs[:, u % 2, 0:KEYS], prcp[:, u % 2:u % 2 + 1], None, ALU.mult).then_inc(s_p, 1)
                if odd:
                    route(pair, 12)
                if mid:
                    lo(s_x2h, i, x2T_lo[:, :, :], psX2[:, 0:D].rearrange("p (c n) -> p c n", c=DC), x2T_hi[:, :, :], s_x2l)
                if odd:
                    route(pair, 13)
                if tail:
                    v.wait_ge(s_z, i - 1)
                    v.scalar_tensor_tensor(out=xt(i - 2), in0=psX[:, D:2 * D], scalar=0.5, in1=xt(i - 2), op0=ALU.mult, op1=ALU.add).then_inc(s_zd, 1)
                if odd:
                    route(pair, 14)
                if nxt:
                    ln1_apply(i + 1, (u + 1) % 2)
                if mid:
                    v.wait_ge(s_gl, i)
                    v.tensor_copy(logit[:, (u - 1) % 2, :], psX2[:, D:D + NE]).then_inc(s_lg, 1)
                    if odd:
                        route(pair, 15)
                    if even:
                        route(pair, 0)
                        route(pair, 1)
                    v.wait_ge(s_th, i)
                    if past(i, 2):
                        v.wait_ge(s_ht, i - 1)
                    v.scalar_tensor_tensor(out=gsil[:], in0=tanh_g[:], scalar=1.0, in1=psG[:, :], op0=ALU.add, op1=ALU.mult).then_inc(s_gs, 1)
                if odd:
                    route(pair, 16)
                if attn:
                    lo(s_ph, i + 1, pT_lo[:, :, :], psPT[:, 0:256].rearrange("p (c n) -> p c n", c=2), pT_hi[:, :, :], s_pl)
                if mid:
                    if even:
                        route(pair, 2)
                    v.wait_ge(s_u, i)
                    v.wait_ge(s_gs, i)
                    v.tensor_tensor(hid[:], gsil[:], psU[:, :], ALU.mult).then_inc(s_h, 1)
                    if even:
                        route(pair, 3)
                    if odd:
                        place(pair)

            def mt(t):
                if isinstance(t, int):
                    return mask_sb[:, t, :]
                return mask_sb[:, bass.ds(t, 1), :].rearrange("p a d -> p (a d)")

            RSTEPS = 17

            def over_e(a):
                return a.unsqueeze(2).to_broadcast([P, 2, NE])

            def route(n, k):
                if k == 0:
                    v.wait_ge(s_lg, 2 * n)
                elif k == 1:
                    v.wait_ge(s_rt, RSTEPS * (n - 1) + 1)
                elif k == 2:
                    v.wait_ge(s_re, n)
                else:
                    v.wait_ge(s_rt, RSTEPS * (n - 1) + k - 1)
                if k == 5 and past(n, 2):
                    v.wait_ge(s_row, 4 * (n - 1))
                s = 0 if k < 11 else 1
                src = score if k < 11 else rest
                if k == 0:
                    v.tensor_reduce(rmax[:], logit[:, :, :], X, ALU.max).then_inc(s_rt, 1)
                elif k == 1:
                    v.tensor_tensor(ex[:, :, :], logit[:, :, :], over_e(rmax[:]), ALU.subtract).then_inc(s_lc, 1)
                elif k == 2:
                    v.tensor_reduce(rsum[:], ex[:, :, :], X, ALU.add).then_inc(s_rt, 1)
                elif k == 3:
                    v.reciprocal(rrcp[:], rsum[:]).then_inc(s_rt, 1)
                elif k == 4:
                    v.tensor_tensor(score[:, :, :], ex[:, :, :], over_e(rrcp[:]), ALU.mult).then_inc(s_rt, 1)
                elif k in (5, 11):
                    v.tensor_reduce(wgt[:, s, :], src[:, :, :], X, ALU.max).then_inc(s_rt, 1)
                elif k in (6, 12):
                    v.tensor_tensor(cand[:, :, :], src[:, :, :], over_e(wgt[:, s, :]), ALU.is_equal).then_inc(s_rt, 1)
                elif k in (7, 13):
                    v.tensor_tensor(cand[:, :, :], cand[:, :, :], desc[:, :, :], ALU.mult).then_inc(s_rt, 1)
                elif k in (8, 14):
                    v.tensor_reduce(first[:], cand[:, :, :], X, ALU.max).then_inc(s_rt, 1)
                elif k in (9, 15):
                    v.tensor_tensor(hot[:, s, :, :], cand[:, :, :], over_e(first[:]), ALU.is_equal).then_inc(s_rt, 1)
                elif k == 10:
                    v.scalar_tensor_tensor(out=rest[:, :, :], in0=hot[:, 0, :, :], scalar=-2.0, in1=score[:, :, :], op0=ALU.mult, op1=ALU.add).then_inc(s_rt, 1)
                elif k == 16:
                    v.tensor_tensor(member[:, :, :], hot[:, 0, :, :], hot[:, 1, :, :], ALU.add).then_inc(s_mem, 1)

            def place(n):
                base = RSTEPS * (n - 1) + 15
                v.wait_ge(s_rk, n)
                v.tensor_tensor(rank[:, :, :], psPT[:, 256:272].rearrange("p (t e) -> p t e", t=2),
                                next_row[:, :].unsqueeze(1).to_broadcast([P, 2, NE]), ALU.add).then_inc(s_rt, 1)
                v.wait_ge(s_rt, base + 1)
                v.tensor_tensor(next_row[:, :], psPT[:, 272:280], next_row[:, :], ALU.add).then_inc(s_rr, 1)
                v.tensor_tensor(rsel[:, :, :, :].rearrange("p s t e -> p s (t e)"), hot[:, :, :, :].rearrange("p s t e -> p s (t e)"),
                                rank[:, :, :].rearrange("p t e -> p (t e)").unsqueeze(1).to_broadcast([P, TOP, 2 * NE]), ALU.mult).then_inc(s_rt, 1)
                v.wait_ge(s_rt, base + 2)
                if past(n, 2):
                    for k in range(4):
                        v.wait_ge(s_sc[k], 16 * (n - 1))
                with nc.allow_low_precision(reason="one row number of each sum, under 2^24, is not 0: exact"):
                    v.tensor_reduce(pos_i[:, :, :], rsel[:, :, :, :], X, ALU.add).then_inc(s_pos, 1)

            v.wait_ge(s_const, NCONST)
            step(0, 0, 0, mid=False, tail=False)
            v.wait_ge(s_x[2], 16)
            ln1_stats(TB, NT)
            v.wait_ge(s_rs1, 2)
            step(1, 1, 0, tail=False)
            step(2, 2, 1)
            step(3, 3, 1)
            v.wait_ge(s_rs1, 3)
            with v.Fori(1, NT // 4 - 1) as q:
                for u in range(4):
                    step(4 * q + u, u, 2 * q + u // 2)
            for i in range(12, NT):
                step(i, i % 4, i // 2, nxt=i + 1 < NT)
            step(16, 0, 8, attn=False, nxt=False)
            for k in range(4, 17):
                route(NT // 2, k)
            place(NT // 2)

            done = [0]

            def chain(ins):
                done[0] += 1
                ins.then_inc(s_tb, 1)
                v.wait_ge(s_tb, done[0])

            v.wait_ge(s_rr, NT // 2)
            chain(v.tensor_tensor(cnt[:], next_row[0:1, :], base_row[:], ALU.subtract))
            v.tensor_copy(fill_i[:], next_row[0:1, :]).then_inc(s_tab, 1)
            chain(v.tensor_tensor(over[:, :, :], cnt[:].unsqueeze(2).to_broadcast([1, NE, NT]), m128[:, :, :], ALU.is_gt))
            chain(v.tensor_reduce(ntile[:], over[:, :, :], X, ALU.add))
            chain(v.tensor_tensor(cumx[:, :, :], ntile[:].unsqueeze(1).to_broadcast([1, NE, NE]), upto[:, :, :], ALU.mult))
            chain(v.tensor_reduce(cum[:], cumx[:, :, :], X, ALU.add))
            chain(v.tensor_tensor(ended, tile_no[:, :, :], cum[:].unsqueeze(1).to_broadcast([1, MAXT, NE]), ALU.is_ge))
            chain(v.tensor_reduce(te[:], ended, X, ALU.add))
            chain(v.tensor_tensor(ended, ended, ntile[:].unsqueeze(1).to_broadcast([1, MAXT, NE]), ALU.mult))
            chain(v.tensor_reduce(tstart[:], ended, X, ALU.add))
            chain(v.tensor_tensor(trow[:], tile_no[:, :, 0], tstart[:], ALU.subtract))
            chain(v.tensor_scalar(trow2[:], te[:], float(REGION), None, ALU.mult))
            chain(v.scalar_tensor_tensor(out=trow2[:], in0=trow[:], scalar=128.0, in1=trow2[:], op0=ALU.mult, op1=ALU.add))
            v.tensor_scalar(te_i[:], te[:], float(NE - 1), None, ALU.min).then_inc(s_tab, 1)
            v.tensor_scalar(trow_i[:], trow2[:], float(FILLER), None, ALU.min).then_inc(s_tab, 1)

            lo(s_hh, NT, hT_lo[:, :, :], psHT[:, :].rearrange("p (c n) -> p c n", c=4), hT_hi[:, :, :], s_hl)
            v.wait_ge(s_lhi, 1)
            v.tensor_tensor(flat(w13_lo, 6), w13_raw(), flat(w13_hi, 6).bitcast(F32), ALU.subtract).then_inc(s_llo, 1)
            for c in range(DC):
                v.wait_ge(s_lhi, 3 + c)
                v.tensor_tensor(w13_lo[:, 7, c, :], w13_raw7[c], w13_hi[:, 7, c, :].bitcast(F32), ALU.subtract).then_inc(s_llo, 1)
            v.wait_ge(s_z, NT)
            v.scalar_tensor_tensor(out=xt(NT - 1), in0=psX[:, D:2 * D], scalar=0.5, in1=xt(NT - 1), op0=ALU.mult, op1=ALU.add).then_inc(s_zd, 1)
            v.wait_ge(s_bias, 16)
            v.wait_ge(s_tab, 3)

            def estep(seen, i, u, q, new=True, up=True, down=True, dest=True):
                if dest:
                    k = (u - 2) % 4
                    if past(i, 6):
                        v.wait_ge(s_ys[k], 16 * (q - 1 if u < 2 else q))
                        if not isinstance(i, int):
                            apart(v, s_pv)
                    v.tensor_copy(dest_row[:, k:k + 1], rin[:, k, D:D + 1].bitcast(I32)).then_inc(s_ix, 1)
                if new:
                    k = u % 2
                    lo(s_eh, i + 1, eT_lo[k][:, :, :], psXe[:, 0:D].rearrange("p (c n) -> p c n", c=DC), eT_hi[k][:, :, :], s_el)
                if down:
                    k = (u - 3) % 2
                    lo(s_heh, i - 2, ehT_lo[k], psHe[:, 0:H].rearrange("p (c n) -> p c n", c=DC), ehT_hi[k], s_hel)
                if up:
                    e = expert_of(v, seen, i, u, 1)
                    v.wait_ge(s_up, i)
                    if past(i, 5):
                        v.wait_ge(s_yo, i - 4)
                    v.tensor_tensor(u13[(u - 1) % 4][:, 0:2 * H], psUe[(u - 1) % 2][:, :],
                                    bias_all[:, bass.ds(e, 1), 0:2 * H].rearrange("p a n -> p (a n)"), ALU.add).then_inc(s_ub, 1)
                if down:
                    e = expert_of(v, seen, i, u, 3)
                    v.wait_ge(s_dn, i - 2)
                    if past(i, 5) and not up:
                        v.wait_ge(s_yo, i - 4)
                    v.tensor_tensor(yb[:, (u - 3) % 2, :], psYe[(u - 3) % 2][:, 0:D],
                                    bias_all[:, bass.ds(e, 1), 2 * H:3 * H].rearrange("p a n -> p (a n)"), ALU.add).then_inc(s_yb, 1)

            seen = {}
            for i in range(8):
                estep(seen, i, i % 4, i // 4, up=i >= 1, down=i >= 3, dest=i >= 2)
            with v.Fori(2, MAXT // 4) as q:
                seen = {}
                for u in range(4):
                    estep(seen, 4 * q + u, u, q)
            seen = {}
            for i in range(MAXT // 4 * 4, MAXT + 3):
                estep(seen, i, i % 4, i // 4, new=i < MAXT, up=i - 1 < MAXT, dest=i - 2 < MAXT)

            for c in range(4):
                v.wait_ge(s_c[c % 3], 32 if c < 3 else 64)
                v.tensor_tensor(x_all[:, 4 * c:4 * c + 4, :], x_all[:, 4 * c:4 * c + 4, :], comb(c)[:, 0], ALU.add).then_inc(s_c1, 1)
                v.wait_ge(s_c1, c + 1)
                v.tensor_tensor(x_all[:, 4 * c:4 * c + 4, :], x_all[:, 4 * c:4 * c + 4, :], comb(c)[:, 1], ALU.add).then_inc(s_c2, 1)

        @block.gpsimd
        def _(g):
            made = [0]

            def make(ins):
                made[0] += 1
                return ins.then_inc(s_const, 1)

            make(g.memset(nhalf[:], -0.5))
            make(g.memset(ident[:], 0.0))
            make(g.memset(ones[:], 1.0))
            make(g.memset(earlier[:], 0.0))
            make(g.memset(fill_blk[:], 0.0))
            make(g.memset(upto[:], 0.0))
            make(g.memset(rows[:, :, D + 1:ROW], 0.0))
            g.wait_ge(s_const, made[0])
            make(g.affine_select(out=ident[:], in_=ident[:], compare_op=ALU.not_equal, fill=1.0, base=0, pattern=[[-1, P]], channel_multiplier=1))
            make(g.affine_select(out=earlier[:], in_=earlier[:], compare_op=ALU.is_ge, fill=1.0, base=0, pattern=[[-1, P]], channel_multiplier=1))
            make(g.affine_select(out=upto[:], in_=upto[:], compare_op=ALU.is_gt, fill=1.0, base=0, pattern=[[-1, NE], [1, NE]], channel_multiplier=0))
            make(g.iota(fill_blk[:, D:D + 1].bitcast(I32), pattern=[[0, 1]], base=SKIP, channel_multiplier=1))
            make(g.iota(dest_i[:], pattern=[[S, B], [1, TB], [T, TOP]], base=0, channel_multiplier=TB))
            make(g.iota(desc[:], pattern=[[0, 2], [-1, NE]], base=NE, channel_multiplier=0, allow_small_or_imprecise_dtypes=True))
            make(g.iota(next_row[:], pattern=[[REGION, NE]], base=0, channel_multiplier=0, allow_small_or_imprecise_dtypes=True))
            make(g.iota(base_row[:], pattern=[[REGION, NE]], base=0, channel_multiplier=0, allow_small_or_imprecise_dtypes=True))
            make(g.iota(m128[:], pattern=[[0, NE], [P, NT]], base=0, channel_multiplier=0, allow_small_or_imprecise_dtypes=True))
            make(g.iota(tile_no[:, :, :], pattern=[[1, MAXT], [0, NE]], base=0, channel_multiplier=0, allow_small_or_imprecise_dtypes=True))
            assert made[0] == NCONST

            def rstd1_of(a, b, n):
                g.wait_ge(s_mv1, b)
                g.tensor_scalar(ve1[:, a:b], mv1[:, a:b, 1], EPS, None, ALU.add).then_inc(s_ve1, 1)
                g.wait_ge(s_ve1, n)
                g.tensor_tensor(rstd1[:, a:b], ve1[:, a:b], nhalf[:, 0:1].to_broadcast([P, b - a]), ALU.pow).then_inc(s_rs1, 1)

            def rstd2_of(n):
                g.wait_ge(s_mv2, n)
                if not isinstance(n, int):
                    apart(g, s_pg)
                g.tensor_scalar(ve2[:], mv2[:, 1:2], EPS, None, ALU.add).then_inc(s_ve2, 1)
                g.wait_ge(s_ve2, n)
                g.tensor_tensor(rstd2[:], ve2[:], nhalf[:], ALU.pow).then_inc(s_rs2, 1)

            def step(i, u, pair):
                rstd2_of(i)
                if u % 2 == 1 and past(i, 3):
                    if not isinstance(i, int) or i < NT - 2:
                        split_lo(pair - 1)
                    dests(pair, i - 3)
                if u % 2 == 0 and past(i, 4):
                    scatter(pair - 1)

            def dests(n, t):
                if past(n, 2):
                    for k in range(4):
                        g.wait_ge(s_sc[k], 16 * (n - 1))
                    apart(g, s_pg)
                d = dest_i[:, t:t + 2, :] if isinstance(t, int) else dest_i[:, bass.ds(t, 2), :]
                g.tensor_copy(rows[:, :, D].bitcast(I32), d.rearrange("p a s -> p (a s)")).then_inc(s_dst, 1)

            def scatter(n):
                g.wait_ge(s_pos, n)
                g.wait_ge(s_dst, n)
                if not isinstance(n, int):
                    g.wait_ge(s_row, 4 * n)
                    apart(g, s_pg)
                for t in range(2):
                    for s in range(TOP):
                        k = 2 * t + s
                        if isinstance(n, int):
                            g.wait_ge(s_row, 4 * (n - 1) + k + 1)
                        g.indirect_dma_start(out=sorted_rows, out_offset=bass.IndirectOffsetOnAxis(ap=pos_i[:, s, t:t + 1], axis=0),
                                             in_=rows[:, k, :], in_offset=None).then_inc(s_sc[k], 16)

            def split_lo(e):
                for k, (wh, wl, raw) in enumerate(((w13_hi, w13_lo, w13_raw()), (w2_hi, w2_lo, w2_raw()))):
                    g.wait_ge(s_ehi, 2 * e + 1 + k)
                    g.tensor_tensor(flat(wl, e), raw, flat(wh, e).bitcast(F32), ALU.subtract).then_inc(s_elo, 1)

            rstd1_of(0, 2, 1)
            rstd1_of(2, TB, 2)
            rstd1_of(TB, NT, 3)
            for i in range(1, 8):
                step(i, i % 4, i // 2)
            with g.Fori(2, NT // 4 - 1) as q:
                for u in range(4):
                    step(4 * q + u, u, 2 * q + u // 2)
            for i in range(12, NT + 1):
                step(i, i % 4, i // 2)
            dests(NT // 2, NT - 2)
            scatter(NT // 2)
            g.wait_ge(s_lhi, 2)
            g.tensor_tensor(flat(w2_lo, 6), w2_raw(), flat(w2_hi, 6).bitcast(F32), ALU.subtract).then_inc(s_llo, 1)
            g.wait_ge(s_lhi, 5)
            g.tensor_tensor(flat(w2_lo, 7), w2_raw7, flat(w2_hi, 7).bitcast(F32), ALU.subtract).then_inc(s_llo, 1)

            def ytail(j, k, n, s):
                g.wait_ge(s_yb, n)
                if s is not None:
                    g.wait_ge(s_ys[k], s)
                g.tensor_tensor(yout[k], yb[:, k % 2, :], u13[k][:, H:2 * H], ALU.mult).then_inc(s_yo, 1)
                g.wait_ge(s_yo, n)
                apart(g, s_pg)
                g.indirect_dma_start(out=expert_out, out_offset=bass.IndirectOffsetOnAxis(ap=dest_row[:, k:k + 1], axis=0),
                                     in_=yout[k], in_offset=None, bounds_check=TOP * T - 1, oob_is_err=False).then_inc(s_ys[k], 16)

            for j in range(4):
                ytail(j, j, j + 1, None)
            with g.Fori(1, 9) as q:
                for k in range(4):
                    ytail(None, k, 4 * q + k + 1, 16 * q)
            for j in range(36, MAXT):
                ytail(j, j % 4, j + 1, 16 * (j // 4))


def kernel(x, ctx_1024, mask_BxSxS2_bk0, L0_xattn_W_attn, L0_ffn_gate_w, L0_ffn_w1, L0_ffn_b1,
           L0_ffn_w2, L0_ffn_b2, L0_ffn_w3, L0_ffn_b3, L0_ffn_sw1, L0_ffn_sw2, L0_ffn_sw3):
    import concourse.bacc as bacc
    import numpy as np
    from concourse.bass_utils import run_bass_kernel_spmd

    w_attn = np.asarray(L0_xattn_W_attn)
    laid = {
        "x": np.asarray(x),
        "enc_t": np.asarray(ctx_1024).transpose(0, 2, 1),
        "mask": np.asarray(mask_BxSxS2_bk0),
        "w_ctx": w_attn[:, :D].T,
        "w_dec": w_attn[:, D:].T,
        "gate_t": np.asarray(L0_ffn_gate_w).T,
        "sw12": np.concatenate([np.asarray(L0_ffn_sw1).T, np.asarray(L0_ffn_sw2).T], axis=1),
        "sw3": np.asarray(L0_ffn_sw3).T,
        "w13": np.concatenate([np.asarray(L0_ffn_w1).transpose(0, 2, 1), np.asarray(L0_ffn_w3).transpose(0, 2, 1)], axis=2),
        "w2": np.asarray(L0_ffn_w2).transpose(0, 2, 1),
        "bias": np.concatenate([np.asarray(L0_ffn_b1), np.asarray(L0_ffn_b3), np.asarray(L0_ffn_b2)], axis=1),
    }
    nc = bacc.Bacc("TRN2", target_bir_lowering=False, num_devices=1)
    arrays = {name: np.ascontiguousarray(a) for name, a in laid.items()}
    args = [nc.dram_tensor(name, a.shape, mybir.dt.from_np(a.dtype), kind="ExternalInput").ap() for name, a in arrays.items()]
    args.append(nc.dram_tensor("out", (B, S, D), F32, kind="ExternalOutput").ap())
    bass_xattn_moe(nc, *args)
    r = run_bass_kernel_spmd(nc, [arrays], core_ids=[0])
    return r.results[0]["out"]
```

```python
from contextlib import ExitStack

import concourse.bass as bass
from concourse import mybir

F32 = mybir.dt.float32
F32R = mybir.dt.float32r
BF16 = mybir.dt.bfloat16
I32 = mybir.dt.int32
U8 = mybir.dt.uint8
ALU = mybir.AluOpType
ACT = mybir.ActivationFunctionType
X = mybir.AxisListType.X

P = 128
B, S, D = 2, 1024, 256
KEYS = 154
T = B * S
NT = T // P
TB = NT // B
DC = D // P
LATE = (12, 13, 14)
NOW = NT - len(LATE)
NE, TOP = 8, 2
H = 256
FI = 512
REGION = T + P
FILLER = NE * REGION
ROW = D + 4
NCONST = 17
MAXT = (T * TOP + NE * (P - 1)) // P
SKIP = 1 << 20
EPS = 1e-5
NEG = -3.0e38


def bass_xattn_moe(nc, x, enc_t, mask, w_ctx, w_dec, gate_t, sw12, sw3, w13, w2, bias, out):
    ctx = ExitStack()
    with ctx:
        def sb(name, shape, dt=F32):
            return ctx.enter_context(nc.sbuf_tensor(name, shape, dt))

        def bank(name):
            return ctx.enter_context(nc.psum_tensor(name, [P, 512], F32))

        def sem(name):
            return ctx.enter_context(nc.semaphore(name))

        sorted_rows = nc.dram_tensor("sorted_rows", [FILLER + P, ROW], F32, kind="Internal").ap()
        expert_out = nc.dram_tensor("expert_out", [TOP * T, D], F32, kind="Internal").ap()

        x_all = sb("x_all", [P, NT, D])
        w13_hi = sb("w13_hi", [P, NE, DC, 2 * H], F32R)
        w13_lo = sb("w13_lo", [P, NE, DC, 2 * H], F32R)
        w2_hi = sb("w2_hi", [P, NE, DC, D], F32R)
        w2_lo = sb("w2_lo", [P, NE, DC, D], F32R)
        sw12_hi = sb("sw12_hi", [P, DC, 2 * FI + NE], F32R)
        sw12_lo = sb("sw12_lo", [P, DC, 2 * FI + NE], F32R)
        sw3_hi = sb("sw3_hi", [P, FI // P, D], F32R)
        sw3_lo = sb("sw3_lo", [P, FI // P, D], F32R)
        bias_all = sb("bias_all", [P, NE, 3 * H])
        stage = sb("stage", [P, 2, 1024])
        gate_raw = sb("gate_raw", [P, DC, NE])
        gate_hi = sw12_hi[:, :, 2 * FI:2 * FI + NE]
        gate_lo = sw12_lo[:, :, 2 * FI:2 * FI + NE]
        mask_words = sb("mask_words", [P, NT * KEYS // 4])
        mask_sb = mask_words[:, :].bitcast(U8).rearrange("p (t k) -> p t k", k=KEYS)
        def att(t, e):
            return t[:, e, :, :].rearrange("p c n -> p (c n)")
        encT_hi = att(w13_hi, 7).rearrange("p (b c k) -> p b c k", b=B, c=DC)
        encT_lo = att(w13_lo, 7).rearrange("p (b c k) -> p b c k", b=B, c=DC)
        encW_hi = att(w13_hi, 6).rearrange("p (b c n) -> p b c n", b=B, c=2)
        encW_lo = att(w13_lo, 6).rearrange("p (b c n) -> p b c n", b=B, c=2)
        wdec_hi = w2_hi[:, 7, :, :]
        wdec_lo = w2_lo[:, 7, :, :]

        ident = sb("ident", [P, P])
        earlier = sb("earlier", [P, P], BF16)
        ones = sb("ones", [P, P], BF16)
        nhalf = sb("nhalf", [P, 1])
        silu_warm = sb("silu_warm", [1, 1])
        desc = sb("desc", [P, 2, NE])
        dest_i = sb("dest_i", [P, NT, TOP], I32)
        fill_blk = sb("fill_blk", [P, ROW])
        next_row = sb("next_row", [P, NE])
        base_row = sb("base_row", [1, NE])
        m128 = sb("m128", [1, NE, NT])
        upto = sb("upto", [1, NE, NE])

        st1 = sb("st1", [P, TB, 6])
        mv1 = sb("mv1", [P, NT, 2])
        ve1 = sb("ve1", [P, NT])
        rstd1 = sb("rstd1", [P, NT])
        st2 = sb("st2", [P, 6])
        mv2 = sb("mv2", [P, 2])
        ve2 = sb("ve2", [P, 1])
        rstd2 = sb("rstd2", [P, 1])
        xn = sb("xn", [P, 2, D])
        xT_hi = sb("xT_hi", [P, DC, P], F32R)
        xT_lo = sb("xT_lo", [P, DC, P], F32R)
        smk = sb("smk", [P, KEYS])
        negmax = sb("negmax", [P, 1])
        probs = sb("probs", [P, 2, D])
        psum_p = sb("psum_p", [P, 2])
        prcp = sb("prcp", [P, 2])
        pT_hi = sb("pT_hi", [P, 2, P], F32R)
        pT_lo = sb("pT_lo", [P, 2, P], F32R)
        xn2 = sb("xn2", [P, 4, D])
        x2T_hi = sb("x2T_hi", [P, DC, P], F32R)
        x2T_lo = sb("x2T_lo", [P, DC, P], F32R)
        tanh_g = sb("tanh_g", [P, FI])
        gsil = sb("gsil", [P, FI])
        hid = sb("hid", [P, FI])
        hT_hi = sb("hT_hi", [P, 4, P], F32R)
        hT_lo = sb("hT_lo", [P, 4, P], F32R)
        logit = sb("logit", [P, 2, NE])
        rmax = sb("rmax", [P, 2])
        ex = sb("ex", [P, 2, NE])
        rsum = sb("rsum", [P, 2])
        rrcp = sb("rrcp", [P, 2])
        score = sb("score", [P, 2, NE])
        cand = sb("cand", [P, 2, NE])
        first = sb("first", [P, 2])
        hot = sb("hot", [P, TOP, 2, NE])
        wgt = sb("wgt", [P, TOP, 2])
        rest = sb("rest", [P, 2, NE])
        member = sb("member", [P, 2, NE], BF16)
        rank = sb("rank", [P, 2, NE])
        rsel = sb("rsel", [P, TOP, 2, NE])
        pos_i = sb("pos_i", [P, TOP, 2], I32)
        rows = sb("rows", [P, 4, ROW])
        cnt = sb("cnt", [1, NE])
        over = sb("over", [1, NE, NT])
        ntile = sb("ntile", [1, NE])
        cumx = sb("cumx", [1, NE, NE])
        cum = sb("cum", [1, NE])
        te = sb("te", [1, MAXT])
        tstart = sb("tstart", [1, MAXT])
        trow = sb("trow", [1, MAXT])
        trow2 = sb("trow2", [1, MAXT])
        te_i = sb("te_i", [1, MAXT], I32)
        trow_i = sb("trow_i", [1, MAXT], I32)
        fill_i = sb("fill_i", [1, NE], I32)
        tile_no = sb("tile_no", [1, MAXT, NE])
        ended = gsil[0:1, 0:MAXT * NE].rearrange("p (j e) -> p j e", e=NE)
        rin = rows
        eT_hi = [x2T_hi[:, :, :], xT_hi[:, :, :]]
        eT_lo = [x2T_lo[:, :, :], xT_lo[:, :, :]]
        ehT_hi = [pT_hi[:, :, :], hT_hi[:, 0:2, :]]
        ehT_lo = [pT_lo[:, :, :], hT_lo[:, 0:2, :]]
        u13 = [tanh_g[:, :], gsil[:, :], hid[:, :], stage[:, 0, 0:512]]
        dest_row = sb("dest_row", [P, 4], I32)
        ehid = xn
        yb = probs
        yout = [xn2[:, 3, :], mask_words[:, 0:D], stage[:, 1, 0:256], stage[:, 1, 256:512]]

        LOGITS = 512 - NE
        U2 = LOGITS - D
        U1 = FI - U2
        psX = bank("psX")
        psX2 = bank("psX2")
        psPT = bank("psPT")
        psHT = bank("psHT")
        psS = bank("psS")
        psG = bank("psG")
        psU = bank("psU")
        psO = bank("psO")
        psXe, psHe = psX2, psHT
        psUe = [psG, psU]
        psYe = [psO, psS]

        late_x = [(xT_hi, xT_lo), (x2T_hi, x2T_lo), (xT_hi, xT_lo)]
        late_sil = [tanh_g[:, :], gsil[:, :], tanh_g[:, :]]
        late_hid = [hid[:, :], stage[:, 0, 0:FI], hid[:, :]]
        late_ps_z = [psS, psO, psS]

        s_const = sem("constants_made")
        s_gh = sem("gate_hi")
        s_x = [sem("x_pair0"), sem("x_batch0"), sem("x_batch1")]
        s_mask = sem("mask_loaded")
        s_gate = sem("gate_loaded")
        s_bias = sem("bias_loaded")
        s_ld = [sem("stage0_loaded"), sem("stage1_loaded")]
        s_shi = sem("setup_hi")
        s_slo = sem("setup_lo")
        s_pad = sem("enc_padded")
        s_ehi = sem("expert_w_hi")
        s_elo = sem("expert_w_lo")
        s_w7 = sem("expert7_loaded")
        s_lhi = sem("late_w_hi")
        s_llo = sem("late_w_lo")
        s_ew = sem("encW_product")
        s_ewh = sem("encW_hi")
        s_ewl = sem("encW_lo")
        s_bn1, s_mv1, s_ve1, s_rs1, s_xn = sem("ln1_stats"), sem("ln1_mv"), sem("ln1_ve"), sem("ln1_rstd"), sem("xn_ready")
        s_bn2, s_mv2, s_ve2, s_rs2, s_xn2 = sem("ln2_stats"), sem("ln2_mv"), sem("ln2_ve"), sem("ln2_rstd"), sem("xn2_ready")
        s_t1, s_xh, s_xl = sem("xT_psum"), sem("xT_hi_ready"), sem("xT_lo_ready")
        s_s, s_sm, s_nm, s_ex, s_rc, s_p = sem("scores"), sem("scores_masked"), sem("negmax_ready"), sem("exp_done"), sem("prcp_ready"), sem("probs_ready")
        s_tp, s_ph, s_pl = sem("pT_psum"), sem("pT_hi_ready"), sem("pT_lo_ready")
        s_o, s_x1 = sem("attn_out"), sem("x1_ready")
        s_t2, s_x2h, s_x2l = sem("x2T_psum"), sem("x2T_hi_ready"), sem("x2T_lo_ready")
        s_gl, s_lg = sem("gate_logits"), sem("logits_copied")
        s_g, s_th, s_gs = sem("ffn_g"), sem("tanh_done"), sem("gsil_ready")
        s_u, s_h = sem("ffn_u"), sem("hidden_ready")
        s_ht, s_hh, s_hl = sem("hT_psum"), sem("hT_hi_ready"), sem("hT_lo_ready")
        s_z, s_zd = sem("ffn_z"), sem("z_added")
        s_rt = sem("route_step")
        s_ps = sem("place_step")
        s_lc = sem("route_shifted")
        s_re = sem("route_exp")
        s_mem = sem("members_ready")
        s_rk = sem("ranks")
        s_rr = sem("ranks_read")
        s_wr = sem("weights_ready")
        s_pos = sem("pos_ready")
        s_row = sem("rows_scaled")
        s_dst = sem("row_destinations")
        s_sc = [sem(f"rows_scattered{k}") for k in range(4)]
        s_tb = sem("table_step")
        s_tab = sem("table_ready")
        s_fill = sem("filler_written")
        s_rin = [sem(f"rin{k}_loaded") for k in range(4)]
        s_te, s_eh, s_el = sem("eT_psum"), sem("eT_hi_ready"), sem("eT_lo_ready")
        s_up, s_ub, s_si = sem("e_up"), sem("e_biased"), sem("e_silu")
        s_the, s_heh, s_hel = sem("ehT_psum"), sem("ehT_hi_ready"), sem("ehT_lo_ready")
        s_ix = sem("dest_rows_copied")
        s_dn, s_yb, s_yo = sem("e_down"), sem("e_y_biased"), sem("e_y_ready")
        s_ys = [sem(f"y_scattered{k}") for k in range(4)]
        s_c = [sem(f"comb{k}_loaded") for k in range(3)]
        s_c1, s_c2, s_c3 = sem("comb_first"), sem("comb_done"), sem("comb_first_tile12")
        s_last = [sem("last_comb_first_loaded"), sem("last_comb_second_loaded")]
        s_out = sem("out_stored")

        s_pv, s_pp, s_pg, s_pa = sem("passed_dve"), sem("passed_pe"), sem("passed_pool"), sem("passed_act")

        block = ctx.enter_context(nc.Block())

        def apart(engine, passed):
            engine.sem_inc(passed, 1)

        def fill(engine, experts):
            engine.wait_ge(s_tab, 1)
            for e in experts:
                r = engine.value_load(fill_i[0:1, e:e + 1], min_val=e * REGION, max_val=e * REGION + T)
                engine.dma_start(sorted_rows[bass.ds(r, P), :], fill_blk[:]).then_inc(s_fill, 16)

        def past_int(i, n):
            return isinstance(i, int) and i >= n

        def past(i, n):
            return not isinstance(i, int) or i >= n

        def tile(t, i):
            if isinstance(i, int):
                return t[:, i, :]
            return t[:, bass.ds(i, 1), :].rearrange("p a d -> p (a d)")

        RSTEPS = 15
        NSET = 5
        wctx_hi = hT_hi[:, :, :].rearrange("p a b -> p (a b)").rearrange("p (c n) -> p c n", c=DC)
        wctx_lo = hT_lo[:, :, :].rearrange("p a b -> p (a b)").rearrange("p (c n) -> p c n", c=DC)

        def setup_parts(n):
            raw = stage[:, n % 2, :]
            if n == 0:
                r = raw[:, 0:B * DC * KEYS].rearrange("p (b c k) -> p b c k", b=B, c=DC)
                return [(r[:, b], encT_hi[:, b, :, 0:KEYS], encT_lo[:, b, :, 0:KEYS]) for b in range(B)]
            if n == 1:
                return [(raw[:, 0:512].rearrange("p (c n) -> p c n", c=DC), wctx_hi, wctx_lo),
                        (raw[:, 512:1024].rearrange("p (c n) -> p c n", c=DC), wdec_hi, wdec_lo)]
            if n < 4:
                return [(raw, sw12_hi[:, n - 2, 0:2 * FI], sw12_lo[:, n - 2, 0:2 * FI])]
            return [(raw, sw3_hi[:, :, :].rearrange("p c n -> p (c n)"), sw3_lo[:, :, :].rearrange("p c n -> p (c n)"))]

        def setup_lo(engine, n):
            engine.wait_ge(s_shi, n + 1)
            for raw, hi, lo in setup_parts(n):
                mm = engine.tensor_tensor(lo, raw, hi.bitcast(F32), ALU.subtract)
            mm.then_inc(s_slo, 1)

        def w13_raw():
            return stage[:, 1, :]

        def w2_raw():
            return stage[:, 0, 0:DC * D]

        def flat(t, e):
            return t[:, bass.ds(e, 1), :, :].rearrange("p a c n -> p (a c n)")

        def comb(c):
            return bias_all[:, :, :].rearrange("p e n -> p (e n)").rearrange("p (k s t d) -> p k s t d", k=3, s=TOP, t=4)[:, c % 3]

        w13_raw7 = [xn[:, :, :].rearrange("p a d -> p (a d)"), probs[:, :, :].rearrange("p a d -> p (a d)")]
        w2_raw7 = mask_words[:, 0:DC * D]

        @block.sync
        def _(sp):
            xv = x.rearrange("b (p t) d -> p b t d", t=TB)
            sp.dma_start(x_all[:, 0:2, :], xv[:, 0, 0:2, :]).then_inc(s_x[0], 16)
            sp.dma_start(stage[:, 0, 0:B * DC * KEYS].rearrange("p (b c k) -> p b c k", b=B, c=DC),
                         enc_t.rearrange("b (c p) k -> p b c k", p=P)).then_inc(s_ld[0], 16)
            sp.dma_start(stage[:, 1, 0:512].rearrange("p (c n) -> p c n", c=DC), w_ctx.rearrange("(c p) n -> p c n", p=P)).then_inc(s_ld[1], 16)
            for c in range(DC):
                sp.wait_ge(s_slo, c + 1)
                sp.dma_start(stage[:, c, :], sw12[c * P:(c + 1) * P, :]).then_inc(s_ld[c], 16)
            sp.dma_start(x_all[:, TB:NT, :], xv[:, 1]).then_inc(s_x[2], 16)
            sp.wait_ge(s_slo, 3)
            sp.dma_start(stage[:, 0, :].rearrange("p (c n) -> p c n", n=D), sw3.rearrange("(c p) n -> p c n", p=P)).then_inc(s_ld[0], 16)

            def load_w13(e):
                sp.dma_start(w13_raw().rearrange("p (c n) -> p c n", c=DC), w13.rearrange("e (c p) n -> p e c n", p=P)[:, bass.ds(e, 1)].rearrange("p a c n -> p (a c) n")).then_inc(s_ld[1], 16)

            def load_w2(e):
                sp.dma_start(w2_raw().rearrange("p (c n) -> p c n", c=DC), w2.rearrange("e (c p) n -> p e c n", p=P)[:, bass.ds(e, 1)].rearrange("p a c n -> p (a c) n")).then_inc(s_ld[0], 16)

            sp.wait_ge(s_slo, 4)
            load_w13(0)
            sp.wait_ge(s_slo, 5)
            load_w2(0)
            with sp.Fori(1, 6) as e:
                sp.wait_ge(s_elo, 2 * e - 1)
                load_w13(e)
                sp.wait_ge(s_elo, 2 * e)
                load_w2(e)
            sp.dma_start(bias_all[:, :, :].rearrange("p e n -> p (e n)"), bias.rearrange("e n -> (e n)").partition_broadcast(P)).then_inc(s_bias, 16)
            sp.wait_ge(s_elo, 11)
            load_w13(6)
            sp.wait_ge(s_elo, 12)
            load_w2(6)
            sp.dma_start(sorted_rows[FILLER:FILLER + P, :], fill_blk[:]).then_inc(s_fill, 16)
            sp.wait_ge(s_tp, NT)
            for c in range(DC):
                sp.dma_start(w13_raw7[c], w13[7, c * P:(c + 1) * P, :]).then_inc(s_w7, 16)
            sp.dma_start(w2_raw7.rearrange("p (c n) -> p c n", c=DC), w2[7].rearrange("(c p) n -> p c n", p=P)).then_inc(s_w7, 16)
            fill(sp, range(5))
            sp.wait_ge(s_fill, 16 * (NE + 1))
            sp.wait_ge(s_tab, 3)
            for k in range(4):
                sp.wait_ge(s_sc[k], 16 * NT // 2)

            def load_rows(j, k, reuse):
                if reuse is not None:
                    sp.wait_ge(s_ix, reuse)
                r = sp.value_load(trow_i[0:1, bass.ds(j, 1)], min_val=0, max_val=FILLER)
                sp.dma_start(rin[:, k, :], sorted_rows[bass.ds(r, P), :]).then_inc(s_rin[k], 16)

            for j in range(4):
                load_rows(j, j, None)
            with sp.Fori(1, 9) as q:
                for k in range(4):
                    load_rows(4 * q + k, k, 4 * q + k - 3)
            for j in range(36, MAXT):
                load_rows(j, j % 4, j - 3)

            for k in range(4):
                sp.wait_ge(s_ys[k], 16 * len(range(k, MAXT, 4)))
            yv = expert_out.rearrange("(s b p t) d -> p s b t d", s=TOP, b=B, t=TB)
            ov = out.rearrange("b (p t) d -> p b t d", t=TB)

            def load_comb(c):
                for s in range(TOP):
                    sp.dma_start(comb(c)[:, s], yv[:, s, c // 2, (c % 2) * 4:(c % 2) * 4 + 4, :]).then_inc(s_c[c] if c < 3 else s_last[s], 16)

            sp.wait_ge(s_yb, MAXT)
            for c in range(3):
                load_comb(c)
            sp.wait_ge(s_c2, 1)
            load_comb(3)
            for n, (t0, t1) in enumerate([(0, 4), (4, 8), (8, 12), (12, 14), (14, 16)]):
                sp.wait_ge(s_c2, n + 1)
                sp.dma_start(ov[:, t0 // TB, t0 % TB:t0 % TB + t1 - t0, :], x_all[:, t0:t1, :]).then_inc(s_out, 16)
            sp.wait_ge(s_out, 5 * 16)

        @block.tensor
        def _(pe):
            def three(o, lh, ll, rh, rl, start, stop):
                pe.matmul(o, lh, rh, start=start, stop=False)
                pe.matmul(o, lh, rl, start=False, stop=False)
                return pe.matmul(o, ll, rh, start=False, stop=stop)

            def enc_w():
                pe.wait_ge(s_pad, 2)
                for b in range(B):
                    for k in range(2):
                        o = [psG, psU][b][:, k * D:(k + 1) * D]
                        for c in range(DC):
                            ks = slice(k * P, (k + 1) * P)
                            mm = three(o, encT_hi[:, b, c, ks], encT_lo[:, b, c, ks], wctx_hi[:, c], wctx_lo[:, c], c == 0, c == DC - 1)
                    mm.then_inc(s_ew, 1)

            def transpose_xn(t, k):
                pe.wait_ge(s_xn, t + 1)
                for c in range(DC):
                    mm = pe.transpose(psX[:, c * P:(c + 1) * P], xn[:, k, c * P:(c + 1) * P], ident[:])
                mm.then_inc(s_t1, 1)

            def batch(t, b):
                if isinstance(b, int):
                    return t[:, b]
                return t[:, bass.ds(b, 1)].rearrange("p a c k -> p (a c) k")

            def transpose_hidden(n):
                pe.wait_ge(s_h, n)
                for c in range(4):
                    mm = pe.transpose(psHT[:, c * P:(c + 1) * P], hid[:, c * P:(c + 1) * P], ident[:])
                mm.then_inc(s_ht, 1)

            def step(i, u4, p, b, attn=True, norm=True, gate=True, ffn=True, last=True, nxt=True, hidden=True):
                u = u4 % 2
                n = NOW if past_int(i, NT + 1) else i - 1

                def first_g():
                    if past(i, 3):
                        pe.wait_ge(s_gs, n - 1)
                    for c in range(DC):
                        mm = three(psG[:, :], x2T_hi[:, c], x2T_lo[:, c], sw12_hi[:, c, 0:FI], sw12_lo[:, c, 0:FI], c == 0, c == DC - 1)
                    mm.then_inc(s_g, 1)

                if attn:
                    pe.wait_ge(s_xl, i + 1)
                    if past(i, 1):
                        pe.wait_ge(s_sm, i)
                    if past(i, 4):
                        pe.wait_ge(s_zd, i - 3)
                    for c in range(DC):
                        mm = three(psS[:, 0:KEYS], xT_hi[:, c], xT_lo[:, c], batch(encT_hi, b)[:, c, 0:KEYS], batch(encT_lo, b)[:, c, 0:KEYS], c == 0, c == DC - 1)
                    mm.then_inc(s_s, 1)
                if gate:
                    pe.wait_ge(s_x2l, i - 1)
                    if ffn and not past_int(i, NT + 1):
                        first_g()
                    w = 0
                    if ffn:
                        w = U2
                        if past(i, 3):
                            pe.wait_ge(s_h, n - 1)
                    cols = slice(2 * FI - w, 2 * FI + NE)
                    for c in range(DC):
                        mm = three(psX2[:, LOGITS - w:LOGITS + NE], x2T_hi[:, c], x2T_lo[:, c], sw12_hi[:, c, cols], sw12_lo[:, c, cols], c == 0, c == DC - 1)
                    mm.then_inc(s_gl, 1)
                if attn:
                    if past(i, 1):
                        pe.wait_ge(s_x1, i)
                    else:
                        pe.wait_ge(s_slo, 2)
                    for c in range(DC):
                        three(psO[:, 0:D], xT_hi[:, c], xT_lo[:, c], wdec_hi[:, c], wdec_lo[:, c], c == 0, False)
                    if not past(i, 1):
                        enc_w()
                if u == 1 and past(i, 5) and not past_int(i, NT + 1):
                    ranks(p - 1)
                if ffn:
                    if past_int(i, NT + 1):
                        first_g()
                        ranks(p)
                    for c in range(DC):
                        mm = three(psU[:, 0:U1], x2T_hi[:, c], x2T_lo[:, c], sw12_hi[:, c, FI:FI + U1], sw12_lo[:, c, FI:FI + U1], c == 0, c == DC - 1)
                    mm.then_inc(s_u, 1)
                if last:
                    pe.wait_ge(s_hl, NOW if past_int(i, NT + 2) else i - 2)
                    if attn:
                        pe.wait_ge(s_sm, i + 1)
                    for c in range(4):
                        mm = three(psS[:, D:2 * D], hT_hi[:, c], hT_lo[:, c], sw3_hi[:, c], sw3_lo[:, c], c == 0, c == 3)
                    mm.then_inc(s_z, 1)
                if attn:
                    pe.wait_ge(s_p, i + 1)
                    for c in range(2):
                        mm = pe.transpose(psPT[:, c * P:(c + 1) * P], probs[:, u, c * P:(c + 1) * P], ident[:])
                    mm.then_inc(s_tp, 1)
                if nxt:
                    if u == 1 and past(i, 5):
                        pe.wait_ge(s_rr, p - 1)
                    transpose_xn(i + 1, 1 - u)
                if norm:
                    pe.wait_ge(s_xn2, i)
                    if gate:
                        pe.wait_ge(s_lg, i - 1)
                    if ffn:
                        pe.wait_ge(s_h, n)
                    x2 = xn2[:, (u4 - 1) % 4, :]
                    for c in range(DC):
                        mm = pe.transpose(psX2[:, c * P:(c + 1) * P], x2[:, c * P:(c + 1) * P], ident[:])
                    mm.then_inc(s_t2, 1)
                if ffn and hidden:
                    transpose_hidden(n)
                if attn:
                    pe.wait_ge(s_pl, i + 1)
                    if not past(i, 1):
                        pe.wait_ge(s_ewl, 2)
                    for c in range(2):
                        mm = three(psO[:, 0:D], pT_hi[:, c], pT_lo[:, c], batch(encW_hi, b)[:, c], batch(encW_lo, b)[:, c], False, c == 1)
                    mm.then_inc(s_o, 1)

            def ranks(n):
                pe.wait_ge(s_mem, n)
                m0, m1 = member[:, 0, :], member[:, 1, :]
                pe.matmul(psX[:, 256:264], earlier[:], m0, start=True, stop=True)
                pe.matmul(psX[:, 264:272], earlier[:], m1, start=True, stop=False)
                pe.matmul(psX[:, 264:272], ones[:], m0, start=False, stop=True)
                pe.matmul(psX[:, 272:280], ones[:], m0, start=True, stop=False)
                pe.matmul(psX[:, 272:280], ones[:], m1, start=False, stop=True).then_inc(s_rk, 1)

            pe.wait_ge(s_const, NCONST)
            transpose_xn(0, 0)
            pe.wait_ge(s_pad, 3)
            pe.wait_ge(s_slo, 1)
            def late_x2T(j):
                pe.wait_ge(s_x2l, NT + j)
                if j == 0:
                    pe.wait_ge(s_lg, NT)
                for c in range(DC):
                    mm = pe.transpose(psX2[:, c * P:(c + 1) * P], xn2[:, j, c * P:(c + 1) * P], ident[:])
                mm.then_inc(s_t2, 1)

            def late_first(j, ps, part, read, done):
                hi, lo = late_x[j]
                pe.wait_ge(s_x2l, NT + j + 1)
                if j > 0:
                    pe.wait_ge(read, NOW + j)
                elif part == 0:
                    pe.wait_ge(s_tab, 1)
                for c in range(DC):
                    cols = slice(part * FI, (part + 1) * FI)
                    mm = three(ps[:, :], hi[:, c], lo[:, c], sw12_hi[:, c, cols], sw12_lo[:, c, cols], c == 0, c == DC - 1)
                mm.then_inc(done, 1)

            def late_g(j):
                late_first(j, psX, 0, s_th, s_g)

            def late_u(j):
                late_first(j, psPT, 1, s_h, s_u)

            step(0, 0, 0, 0, norm=False, gate=False, ffn=False, last=False)
            step(1, 1, 0, 0, gate=False, ffn=False, last=False)
            pe.wait_ge(s_slo, 4)
            pe.wait_ge(s_gate, 17)
            step(2, 2, 1, 0, last=False)
            pe.wait_ge(s_slo, 5)
            step(3, 3, 1, 0)
            with pe.Fori(1, NT // 4 - 1) as q:
                for u in range(4):
                    step(4 * q + u, u, 2 * q + u // 2, q - 1)
            for i in range(12, NT):
                step(i, i % 4, i // 2, 1, ffn=i - 2 < LATE[0], last=i - 3 < LATE[0], nxt=i + 1 < NT)
            step(16, 0, 8, 1, attn=False, ffn=False, last=False, nxt=False)
            ranks(NT // 2 - 1)
            step(17, 1, 8, 1, attn=False, norm=False, last=False, nxt=False, hidden=False)
            transpose_hidden(NOW)
            late_x2T(0)
            late_g(0)
            step(18, 2, 9, 1, attn=False, norm=False, gate=False, ffn=False, nxt=False)
            late_u(0)

            pe.wait_ge(s_tab, 3)

            expert_reg = [pe.alloc_register(f"expert_of_tile{k}") for k in range(4)]

            def estep(i, u, q, new=True, up=True, down=True):
                if down:
                    pe.wait_ge(s_si, i - 2)
                    for c in range(DC):
                        mm = pe.transpose(psHe[:, c * P:(c + 1) * P], ehid[:, (u - 3) % 2, c * P:(c + 1) * P], ident[:])
                    mm.then_inc(s_the, 1)
                if new:
                    k = u % 4
                    pe.wait_ge(s_rin[k], 16 * (q + 1))
                    if past(i, 1):
                        pe.wait_ge(s_el, i)
                    for c in range(DC):
                        mm = pe.transpose(psXe[:, c * P:(c + 1) * P], rin[:, k, c * P:(c + 1) * P], ident[:])
                    mm.then_inc(s_te, 1)
                elif up:
                    pe.wait_ge(s_el, i)
                if up:
                    if isinstance(i, int) and i == 1:
                        pe.wait_ge(s_llo, 5)
                        apart(pe, s_pp)
                    k, k4 = (u - 1) % 2, (u - 1) % 4
                    if not (isinstance(i, int) and i == 1):
                        pe.reg_load(expert_reg[k4], te_i[0:1, bass.ds(i - 1, 1)])
                    e = pe.snap(expert_reg[k4], min_val=0, max_val=NE - 1)
                    wh = w13_hi[:, bass.ds(e, 1)].rearrange("p a c n -> p (a c) n")
                    wl = w13_lo[:, bass.ds(e, 1)].rearrange("p a c n -> p (a c) n")
                    for c in range(DC):
                        mm = three(psUe[k][:, :], eT_hi[k][:, c], eT_lo[k][:, c], wh[:, c], wl[:, c], c == 0, c == DC - 1)
                    mm.then_inc(s_up, 1)
                if down:
                    k = (u - 3) % 2
                    e = pe.snap(expert_reg[(u - 3) % 4], min_val=0, max_val=NE - 1)
                    wh = w2_hi[:, bass.ds(e, 1)].rearrange("p a c n -> p (a c) n")
                    wl = w2_lo[:, bass.ds(e, 1)].rearrange("p a c n -> p (a c) n")
                    pe.wait_ge(s_hel, i - 2)
                    for c in range(DC):
                        mm = three(psYe[k][:, 0:D], ehT_hi[k][:, c], ehT_lo[k][:, c], wh[:, c], wl[:, c], c == 0, c == DC - 1)
                    mm.then_inc(s_dn, 1)

            pe.reg_load(expert_reg[0], te_i[0:1, 0:1])
            for i in range(8):
                estep(i, i % 4, i // 4, up=i >= 1, down=i >= 3)
            with pe.Fori(1, MAXT // 8) as q:
                for u in range(8):
                    estep(8 * q + u, u % 4, 2 * q + u // 4)
            for i in range(MAXT // 8 * 8, MAXT + 3):
                estep(i, i % 4, i // 4, new=i < MAXT, up=i - 1 < MAXT)

            def late_hT(j):
                pe.wait_ge(s_h, NOW + j + 1)
                for c in range(4):
                    mm = pe.transpose(psHT[:, c * P:(c + 1) * P], late_hid[j][:, c * P:(c + 1) * P], ident[:])
                mm.then_inc(s_ht, 1)

            def late_z(j):
                pe.wait_ge(s_hl, NOW + j + 1)
                pe.wait_ge(s_yb, MAXT)
                if j > 1:
                    pe.wait_ge(s_zd, NOW + j - 1)
                for c in range(4):
                    mm = three(late_ps_z[j][:, 0:D], hT_hi[:, c], hT_lo[:, c], sw3_hi[:, c], sw3_lo[:, c], c == 0, c == 3)
                mm.then_inc(s_z, 1)

            late_x2T(1)
            late_x2T(2)
            late_g(1)
            late_hT(0)
            late_u(1)
            late_z(0)
            late_g(2)
            late_hT(1)
            late_u(2)
            late_z(1)
            late_hT(2)
            late_z(2)

        @block.scalar
        def _(act):
            xv = x.rearrange("b (p t) d -> p b t d", t=TB)
            act.dma_start(stage[:, 1, 512:1024].rearrange("p (c n) -> p c n", c=DC), w_dec.rearrange("(c p) n -> p c n", p=P)).then_inc(s_ld[1], 16)
            act.dma_start(mask_sb[:, :, :].rearrange("p (b t) k -> p b (t k)", b=B), mask.rearrange("b (p t) k -> p b (t k)", t=TB)).then_inc(s_mask, 16)
            act.dma_start(x_all[:, 2:TB, :], xv[:, 0, 2:TB, :]).then_inc(s_x[1], 16)
            act.dma_start(gate_raw[:], gate_t.rearrange("(c p) e -> p c e", p=P)).then_inc(s_gate, 16)

            def setup(n):
                act.wait_ge(s_ld[n % 2], [16, 32, 32, 48, 48][n])
                for raw, hi, _ in setup_parts(n):
                    mm = act.activation(hi, raw, ACT.Copy)
                mm.then_inc(s_shi, 1)

            def evac(done, t, out, ps, ready):
                act.wait_ge(done, t)
                act.activation(out, ps, ACT.Copy).then_inc(ready, 1)

            def evac_xT(t):
                evac(s_t1, t + 1, xT_hi[:, :, :], psX[:, 0:D].rearrange("p (c n) -> p c n", c=DC), s_xh)

            def evac_hT(n):
                evac(s_ht, n, hT_hi[:, :, :], psHT[:, :].rearrange("p (c n) -> p c n", c=4), s_hh)

            def step(i, u, p, attn=True, norm=True, ffn=True, nxt=True, hidden=True):
                n = NOW if past_int(i, NT + 1) else i - 1
                if attn:
                    act.wait_ge(s_nm, i + 1)
                    if past(i, 2):
                        act.wait_ge(s_tp, i - 1)
                    act.activation(probs[:, u, 0:KEYS], smk[:], ACT.Exp, bias=negmax[:, 0:1],
                                   accum_out=psum_p[:, u:u + 1]).then_inc(s_ex, 1)
                if attn and not past(i, 1):
                    setup(2)
                    for b in range(B):
                        act.wait_ge(s_ew, b + 1)
                        act.activation(encW_hi[:, b].rearrange("p c n -> p (c n)"), [psG, psU][b][:, :], ACT.Copy).then_inc(s_ewh, 1)
                if u == 1 and past(i, 3):
                    act.wait_ge(s_lc, p)
                    act.activation(ex[:, :, :], ex[:, :, :], ACT.Exp).then_inc(s_re, 1)
                if ffn:
                    act.wait_ge(s_g, n)
                    if past(i, 3):
                        act.wait_ge(s_gs, n - 1)
                    act.activation(tanh_g[:], psG[:, :], ACT.Tanh, scale=0.5).then_inc(s_th, 1)
                if attn:
                    evac(s_tp, i + 1, pT_hi[:, :, :], psPT[:, 0:256].rearrange("p (c n) -> p c n", c=2), s_ph)
                if nxt:
                    evac_xT(i + 1)
                if norm:
                    evac(s_t2, i, x2T_hi[:, :, :], psX2[:, 0:D].rearrange("p (c n) -> p c n", c=DC), s_x2h)
                if ffn and hidden:
                    evac_hT(n)
                if u == 0 and past(i, 4):
                    scale(p - 1, i % 4)
                if u == 1 and past(i, 3) and not past_int(i, 14):
                    split_hi(p - 1)

            def split_hi(e):
                for k, (wh, raw) in ((1, (w13_hi, w13_raw())), (0, (w2_hi, w2_raw()))):
                    act.wait_ge(s_ld[k], 16 * (e + 4))
                    act.activation(flat(wh, e), raw, ACT.Copy).then_inc(s_ehi, 1)

            def scale(n, slot):
                act.wait_ge(s_rt, RSTEPS * (n - 1) + 11)
                if past(n, 2):
                    for k in range(4):
                        act.wait_ge(s_sc[k], 16 * (n - 1))
                if not isinstance(n, int):
                    apart(act, s_pa)
                for t in range(2):
                    for c in range(TOP):
                        k = 2 * t + c
                        act.activation(rows[:, k, 0:D], tile(xn2, slot + t), ACT.Copy, scale=wgt[:, c, t:t + 1]).then_inc(s_row, 1)

            setup(0)
            evac_xT(0)
            setup(1)
            step(0, 0, 0, norm=False, ffn=False)
            setup(3)
            step(1, 1, 0, ffn=False)
            setup(4)
            step(2, 0, 1)
            for i in range(3, 6):
                step(i, i % 2, i // 2)
            with act.Fori(3, NT // 2 - 1) as p:
                for u in range(2):
                    step(2 * p + u, u, p)
            step(14, 0, 7, ffn=False)
            step(15, 1, 7, ffn=False, nxt=False)
            step(16, 0, 8, attn=False, ffn=False, nxt=False)
            step(17, 1, 8, attn=False, norm=False, nxt=False, hidden=False)
            scale(NT // 2, (NT - 2) % 4)

            def late_x2T(j):
                evac(s_t2, NT + j + 1, late_x[j][0][:, :, :], psX2[:, 0:D].rearrange("p (c n) -> p c n", c=DC), s_x2h)

            act.wait_ge(s_o, NT)
            act.wait_ge(s_ld[1], 16 * 10)
            act.activation(flat(w13_hi, 6), w13_raw(), ACT.Copy).then_inc(s_lhi, 1)
            act.wait_ge(s_ld[0], 16 * 10)
            act.activation(flat(w2_hi, 6), w2_raw(), ACT.Copy).then_inc(s_lhi, 1)
            fill(act, range(5, NE))
            late_x2T(0)
            evac_hT(NOW)
            act.wait_ge(s_w7, 48)
            for c in range(DC):
                act.activation(w13_hi[:, 7, c, :], w13_raw7[c], ACT.Copy).then_inc(s_lhi, 1)
            act.activation(flat(w2_hi, 7), w2_raw7, ACT.Copy).then_inc(s_lhi, 1)
            act.activation(silu_warm[:], nhalf[0:1, :], ACT.Silu)

            def estep(i, u, q, new=True, up=True, down=True):
                if down:
                    k = (u - 3) % 2
                    evac(s_the, i - 2, ehT_hi[k], psHe[:, 0:H].rearrange("p (c n) -> p c n", c=DC), s_heh)
                if new:
                    k = u % 2
                    evac(s_te, i + 1, eT_hi[k][:, :, :], psXe[:, 0:D].rearrange("p (c n) -> p c n", c=DC), s_eh)
                if up:
                    act.wait_ge(s_ub, i)
                    act.activation(ehid[:, (u - 1) % 2, :], u13[(u - 1) % 4][:, 0:H], ACT.Silu).then_inc(s_si, 1)

            for i in range(8):
                estep(i, i % 4, i // 4, up=i >= 1, down=i >= 3)
            with act.Fori(1, MAXT // 8) as q:
                for u in range(8):
                    estep(8 * q + u, u % 4, 2 * q + u // 4)
            for i in range(MAXT // 8 * 8, MAXT + 3):
                estep(i, i % 4, i // 4, new=i < MAXT, up=i - 1 < MAXT)

            def late_silu(j):
                act.wait_ge(s_g, NOW + j + 1)
                if j < 2:
                    act.wait_ge(s_yo, MAXT - 2 + j)
                else:
                    act.wait_ge(s_h, NOW + j - 1)
                act.activation(late_sil[j], psX[:, :], ACT.Silu).then_inc(s_th, 1)

            late_silu(0)
            late_x2T(1)
            late_x2T(2)
            evac_hT(NOW + 1)
            late_silu(1)
            evac_hT(NOW + 2)
            late_silu(2)
            evac_hT(NOW + 3)

        @block.vector
        def _(v):
            for t in (encT_hi, encT_lo):
                v.memset(t.bitcast(F32)[:, :, :, KEYS:256], 0.0).then_inc(s_pad, 1)
            v.memset(probs[:, :, KEYS:256], 0.0).then_inc(s_pad, 1)

            def ln1_stats(a, b):
                for t in range(a, b):
                    v.bn_stats(st1[:, t % TB, :], x_all[:, t, :]).then_inc(s_bn1, 1)
                v.wait_ge(s_bn1, b)
                for t in range(a, b):
                    v.bn_aggr(mv1[:, t, :], st1[:, t % TB, :]).then_inc(s_mv1, 1)

            def ln1_apply(t, k):
                if past(t, 2):
                    v.wait_ge(s_t1, t - 1)
                m, r = ((mv1[:, t, 0:1], rstd1[:, t:t + 1]) if isinstance(t, int) else
                        (mv1[:, bass.ds(t, 1), 0:1].rearrange("p a b -> p (a b)"), rstd1[:, bass.ds(t, 1)]))
                v.tensor_scalar(xn[:, k, :], xt(t), m, r, ALU.subtract, ALU.mult).then_inc(s_xn, 1)

            def xt(t):
                return tile(x_all, t)

            def setup(n):
                setup_lo(v, n)

            def lo(ready_hi, n, out, ps, hi, ready):
                v.wait_ge(ready_hi, n)
                v.tensor_tensor(out, ps, hi.bitcast(F32), ALU.subtract).then_inc(ready, 1)

            def lo_xT(t):
                lo(s_xh, t + 1, xT_lo[:, :, :], psX[:, 0:D].rearrange("p (c n) -> p c n", c=DC), xT_hi[:, :, :], s_xl)

            def lo_hT(n):
                lo(s_hh, n, hT_lo[:, :, :], psHT[:, :].rearrange("p (c n) -> p c n", c=4), hT_hi[:, :, :], s_hl)

            def add_z(t, n):
                v.wait_ge(s_z, n)
                v.scalar_tensor_tensor(out=xt(t), in0=psS[:, D:2 * D], scalar=0.5, in1=xt(t), op0=ALU.mult, op1=ALU.add).then_inc(s_zd, 1)

            def gated(n):
                v.wait_ge(s_th, n)
                v.scalar_tensor_tensor(out=gsil[:], in0=tanh_g[:], scalar=1.0, in1=psG[:, :], op0=ALU.add, op1=ALU.mult).then_inc(s_gs, 1)

            def hidden(n):
                v.wait_ge(s_u, n)
                v.wait_ge(s_gs, n)
                if past(n, 2):
                    v.wait_ge(s_ht, n - 1)
                v.tensor_tensor(hid[:, 0:U1], gsil[:, 0:U1], psU[:, 0:U1], ALU.mult)
                v.tensor_tensor(hid[:, U1:FI], gsil[:, U1:FI], psX2[:, LOGITS - U2:LOGITS], ALU.mult).then_inc(s_h, 1)

            def enc_w_lo():
                for b in range(B):
                    v.wait_ge(s_ewh, b + 1)
                    v.tensor_tensor(encW_lo[:, b].rearrange("p c n -> p (c n)"), [psG, psU][b][:, :],
                                    encW_hi[:, b].rearrange("p c n -> p (c n)").bitcast(F32), ALU.subtract).then_inc(s_ewl, 1)

            def step(i, u, p, attn=True, norm=True, gate=True, ffn=True, last=True, nxt=True):
                n = i - 1
                begun = u == 1 and past(i, 3)
                later = u == 0 and past(i, 4)
                if norm:
                    v.wait_ge(s_o, i)
                    v.tensor_tensor(xt(i - 1), psO[:, 0:D], xt(i - 1), ALU.add).then_inc(s_x1, 1)
                    if later:
                        route(p - 1, 5)
                if last:
                    lo_hT(i - 2)
                if norm:
                    v.wait_ge(s_x1, i)
                    if not isinstance(i, int):
                        apart(v, s_pv)
                    v.bn_stats(st2[:], xt(i - 1)).then_inc(s_bn2, 1)
                    if later:
                        route(p - 1, 6)
                    v.wait_ge(s_bn2, i)
                    if not isinstance(i, int):
                        apart(v, s_pv)
                    v.bn_aggr(mv2[:], st2[:]).then_inc(s_mv2, 1)
                if attn:
                    v.wait_ge(s_s, i + 1)
                    if past(i, 1):
                        v.wait_ge(s_ex, i)
                    v.scalar_tensor_tensor(out=smk[:], in0=mt(i), scalar=NEG, in1=psS[:, 0:KEYS], op0=ALU.mult, op1=ALU.add).then_inc(s_sm, 1)
                    if later:
                        route(p - 1, 7)
                    v.wait_ge(s_sm, i + 1)
                    v.tensor_reduce(negmax[:], smk[:], X, ALU.max, negate=True).then_inc(s_nm, 1)
                    if nxt and past(i, 1):
                        ln1_apply(i + 1, 1 - u)
                elif later:
                    route(p - 1, 7)
                if later:
                    route(p - 1, 8)
                if gate:
                    v.wait_ge(s_gl, i - 1)
                    v.tensor_copy(logit[:, u, :], psX2[:, LOGITS:LOGITS + NE]).then_inc(s_lg, 1)
                if begun:
                    route(p, 0)
                if attn:
                    v.wait_ge(s_ex, i + 1)
                    v.reciprocal(prcp[:, u:u + 1], psum_p[:, u:u + 1]).then_inc(s_rc, 1)
                    if begun:
                        route(p, 1)
                    if later:
                        route(p - 1, 9)
                    v.wait_ge(s_rc, i + 1)
                    v.tensor_scalar(probs[:, u, 0:KEYS], probs[:, u, 0:KEYS], prcp[:, u:u + 1], None, ALU.mult).then_inc(s_p, 1)
                elif begun:
                    route(p, 1)
                elif later:
                    route(p - 1, 9)
                if later:
                    route(p - 1, 10)
                placed = u == 1 and past(i, 5) and not past_int(i, NT + 1)
                if placed:
                    place_all(p - 1)
                if ffn:
                    gated(n)
                if norm:
                    v.wait_ge(s_rs2, i)
                    if u == 1 and past(i, 5):
                        v.wait_ge(s_row, 4 * (p - 1))
                    v.tensor_scalar(tile(xn2, (i - 1) % 4), xt(i - 1), mv2[:, 0:1], rstd2[:, 0:1], ALU.subtract, ALU.mult).then_inc(s_xn2, 1)
                if ffn:
                    hidden(n)
                if placed:
                    place_row(p - 1)
                if later:
                    route(p - 1, 11)
                if attn and not past(i, 1):
                    v.wait_ge(s_x[1], 16)
                    ln1_stats(2, TB)
                    enc_w_lo()
                if nxt and not past(i, 1):
                    ln1_apply(1, 1)
                if isinstance(i, int) and i in (1, 2):
                    ln1_stats(TB * (i + 1) // 2, TB * (i + 2) // 2)
                if later:
                    route(p - 1, 12)
                if begun:
                    route(p, 2)
                if later:
                    route(p - 1, 13)
                if attn:
                    lo(s_ph, i + 1, pT_lo[:, :, :], psPT[:, 0:256].rearrange("p (c n) -> p c n", c=2), pT_hi[:, :, :], s_pl)
                if begun:
                    route(p, 3)
                if nxt:
                    lo_xT(i + 1)
                if later:
                    route(p - 1, 14)
                if last:
                    add_z(i - 3, i - 2)
                if begun:
                    route(p, 4)
                if norm:
                    lo(s_x2h, i, x2T_lo[:, :, :], psX2[:, 0:D].rearrange("p (c n) -> p c n", c=DC), x2T_hi[:, :, :], s_x2l)
                if later:
                    route(p - 1, 15)
                if later:
                    route(p - 1, 16)
            def mt(t):
                return tile(mask_sb, t)

            def over_e(a):
                return a.unsqueeze(2).to_broadcast([P, 2, NE])

            def route(n, k):
                if k == 0:
                    v.wait_ge(s_lg, 2 * n)
                elif k == 1:
                    v.wait_ge(s_rt, RSTEPS * (n - 1) + 1)
                elif k == 2:
                    v.wait_ge(s_re, n)
                else:
                    v.wait_ge(s_rt, RSTEPS * (n - 1) + k - 1)
                if k == 5 and past(n, 2):
                    v.wait_ge(s_row, 4 * (n - 1))
                s = 0 if k < 11 else 1
                src = score if k < 11 else rest
                if k == 0:
                    v.tensor_reduce(rmax[:], logit[:, :, :], X, ALU.max).then_inc(s_rt, 1)
                elif k == 1:
                    v.tensor_tensor(ex[:, :, :], logit[:, :, :], over_e(rmax[:]), ALU.subtract).then_inc(s_lc, 1)
                elif k == 2:
                    v.tensor_reduce(rsum[:], ex[:, :, :], X, ALU.add).then_inc(s_rt, 1)
                elif k == 3:
                    v.reciprocal(rrcp[:], rsum[:]).then_inc(s_rt, 1)
                elif k == 4:
                    v.tensor_tensor(score[:, :, :], ex[:, :, :], over_e(rrcp[:]), ALU.mult).then_inc(s_rt, 1)
                elif k in (5, 11):
                    v.tensor_reduce(wgt[:, s, :], src[:, :, :], X, ALU.max).then_inc(s_rt, 1)
                elif k in (6, 12):
                    v.tensor_tensor(cand[:, :, :], src[:, :, :], over_e(wgt[:, s, :]), ALU.is_equal).then_inc(s_rt, 1)
                elif k in (7, 13):
                    v.tensor_tensor(cand[:, :, :], cand[:, :, :], desc[:, :, :], ALU.mult).then_inc(s_rt, 1)
                elif k in (8, 14):
                    v.tensor_reduce(first[:], cand[:, :, :], X, ALU.max).then_inc(s_rt, 1)
                elif k in (9, 15):
                    v.tensor_tensor(hot[:, s, :, :], cand[:, :, :], over_e(first[:]), ALU.is_equal).then_inc(s_rt, 1)
                elif k == 10:
                    v.scalar_tensor_tensor(out=rest[:, :, :], in0=hot[:, 0, :, :], scalar=-2.0, in1=score[:, :, :], op0=ALU.mult, op1=ALU.add).then_inc(s_rt, 1)
                elif k == 16:
                    v.tensor_tensor(member[:, :, :], hot[:, 0, :, :], hot[:, 1, :, :], ALU.add).then_inc(s_mem, 1)

            def place(n):
                place_all(n)
                place_row(n)

            def place_all(n):
                v.wait_ge(s_rk, n)
                v.tensor_tensor(rank[:, :, :], psX[:, 256:272].rearrange("p (t e) -> p t e", t=2),
                                next_row[:, :].unsqueeze(1).to_broadcast([P, 2, NE]), ALU.add).then_inc(s_ps, 1)
                v.wait_ge(s_ps, 2 * n - 1)
                v.tensor_tensor(next_row[:, :], psX[:, 272:280], next_row[:, :], ALU.add).then_inc(s_rr, 1)

            def place_row(n):
                v.tensor_tensor(rsel[:, :, :, :].rearrange("p s t e -> p s (t e)"), hot[:, :, :, :].rearrange("p s t e -> p s (t e)"),
                                rank[:, :, :].rearrange("p t e -> p (t e)").unsqueeze(1).to_broadcast([P, TOP, 2 * NE]), ALU.mult).then_inc(s_ps, 1)
                v.wait_ge(s_ps, 2 * n)
                if past(n, 2):
                    for k in range(4):
                        v.wait_ge(s_sc[k], 16 * (n - 1))
                with nc.allow_low_precision(reason="one row number of each sum, under 2^24, is not 0: exact"):
                    v.tensor_reduce(pos_i[:, :, :], rsel[:, :, :, :], X, ALU.add).then_inc(s_pos, 1)

            v.wait_ge(s_x[0], 16)
            ln1_stats(0, 2)
            setup(0)
            v.wait_ge(s_rs1, 1)
            ln1_apply(0, 0)
            v.wait_ge(s_const, NCONST)
            lo_xT(0)
            setup(1)
            v.wait_ge(s_mask, 16)
            step(0, 0, 0, norm=False, gate=False, ffn=False, last=False)
            v.wait_ge(s_gate, 16)
            v.tensor_copy(gate_hi[:, :, :], gate_raw[:, :, :]).then_inc(s_gh, 1)
            v.wait_ge(s_gh, 1)
            v.tensor_tensor(gate_lo[:, :, :], gate_raw[:, :, :], gate_hi[:, :, :].bitcast(F32), ALU.subtract).then_inc(s_gate, 1)
            v.wait_ge(s_rs1, 2)
            v.wait_ge(s_x[2], 16)
            step(1, 1, 0, gate=False, ffn=False, last=False)
            step(2, 0, 1, last=False)
            for i in range(3, 6):
                step(i, i % 2, i // 2)
            v.wait_ge(s_rs1, 3)
            with v.Fori(3, NT // 2 - 1) as p:
                for u in range(2):
                    step(2 * p + u, u, p)
            step(14, 0, 7, ffn=False)
            step(15, 1, 7, ffn=False, last=False, nxt=False)
            step(16, 0, 8, attn=False, ffn=False, last=False, nxt=False)
            place(NT // 2 - 1)
            step(17, 1, 8, attn=False, norm=False, ffn=False, last=False, nxt=False)
            for k in range(5, 17):
                route(NT // 2, k)
            place(NT // 2)

            done = [0]

            def chain(ins):
                done[0] += 1
                ins.then_inc(s_tb, 1)
                v.wait_ge(s_tb, done[0])

            def late_lo(j):
                lo(s_x2h, NT + j + 1, late_x[j][1][:, :, :], psX2[:, 0:D].rearrange("p (c n) -> p c n", c=DC), late_x[j][0][:, :, :], s_x2l)

            v.wait_ge(s_rr, NT // 2)
            chain(v.tensor_tensor(cnt[:], next_row[0:1, :], base_row[:], ALU.subtract))
            v.tensor_copy(fill_i[:], next_row[0:1, :]).then_inc(s_tab, 1)
            chain(v.tensor_tensor(over[:, :, :], cnt[:].unsqueeze(2).to_broadcast([1, NE, NT]), m128[:, :, :], ALU.is_gt))
            gated(NOW)
            chain(v.tensor_reduce(ntile[:], over[:, :, :], X, ALU.add))
            chain(v.tensor_tensor(cumx[:, :, :], ntile[:].unsqueeze(1).to_broadcast([1, NE, NE]), upto[:, :, :], ALU.mult))
            hidden(NOW)
            chain(v.tensor_reduce(cum[:], cumx[:, :, :], X, ALU.add))
            chain(v.tensor_tensor(ended, tile_no[:, :, :], cum[:].unsqueeze(1).to_broadcast([1, MAXT, NE]), ALU.is_ge))
            chain(v.tensor_reduce(te[:], ended, X, ALU.add))
            chain(v.tensor_tensor(ended, ended, ntile[:].unsqueeze(1).to_broadcast([1, MAXT, NE]), ALU.mult))
            chain(v.tensor_reduce(tstart[:], ended, X, ALU.add))
            late_lo(0)
            chain(v.tensor_tensor(trow[:], tile_no[:, :, 0], tstart[:], ALU.subtract))
            chain(v.tensor_scalar(trow2[:], te[:], float(REGION), None, ALU.mult))
            chain(v.scalar_tensor_tensor(out=trow2[:], in0=trow[:], scalar=128.0, in1=trow2[:], op0=ALU.mult, op1=ALU.add))
            v.tensor_scalar(te_i[:], te[:], float(NE - 1), None, ALU.min).then_inc(s_tab, 1)
            v.tensor_scalar(trow_i[:], trow2[:], float(FILLER), None, ALU.min).then_inc(s_tab, 1)

            lo_hT(NOW)
            v.wait_ge(s_lhi, 1)
            v.tensor_tensor(flat(w13_lo, 6), w13_raw(), flat(w13_hi, 6).bitcast(F32), ALU.subtract).then_inc(s_llo, 1)
            for c in range(DC):
                v.wait_ge(s_lhi, 3 + c)
                v.tensor_tensor(w13_lo[:, 7, c, :], w13_raw7[c], w13_hi[:, 7, c, :].bitcast(F32), ALU.subtract).then_inc(s_llo, 1)
            add_z(NT - 1, NOW)
            v.wait_ge(s_bias, 16)
            v.wait_ge(s_tab, 3)

            expert_reg = [v.alloc_register(f"expert_of_tile{k}") for k in range(4)]

            def estep(i, u, q, new=True, up=True, down=True, dest=True):
                if dest:
                    k = (u - 2) % 4
                    if past(i, 6):
                        v.wait_ge(s_ys[k], 16 * (q - 1 if u < 2 else q))
                        if not isinstance(i, int):
                            apart(v, s_pv)
                    v.tensor_copy(dest_row[:, k:k + 1], rin[:, k, D:D + 1].bitcast(I32)).then_inc(s_ix, 1)
                if down:
                    k = (u - 3) % 2
                    lo(s_heh, i - 2, ehT_lo[k], psHe[:, 0:H].rearrange("p (c n) -> p c n", c=DC), ehT_hi[k], s_hel)
                if new:
                    k = u % 2
                    lo(s_eh, i + 1, eT_lo[k][:, :, :], psXe[:, 0:D].rearrange("p (c n) -> p c n", c=DC), eT_hi[k][:, :, :], s_el)
                if up:
                    k = (u - 1) % 4
                    v.reg_load(expert_reg[k], te_i[0:1, bass.ds(i - 1, 1)])
                    e = v.snap(expert_reg[k], min_val=0, max_val=NE - 1)
                    v.wait_ge(s_up, i)
                    if past(i, 5):
                        v.wait_ge(s_yo, i - 4)
                    v.tensor_tensor(u13[(u - 1) % 4][:, 0:2 * H], psUe[(u - 1) % 2][:, :],
                                    bias_all[:, bass.ds(e, 1), 0:2 * H].rearrange("p a n -> p (a n)"), ALU.add).then_inc(s_ub, 1)
                if down:
                    e = v.snap(expert_reg[(u - 3) % 4], min_val=0, max_val=NE - 1)
                    v.wait_ge(s_dn, i - 2)
                    if past(i, 5) and not up:
                        v.wait_ge(s_yo, i - 4)
                    v.tensor_tensor(yb[:, (u - 3) % 2, :], psYe[(u - 3) % 2][:, 0:D],
                                    bias_all[:, bass.ds(e, 1), 2 * H:3 * H].rearrange("p a n -> p (a n)"), ALU.add).then_inc(s_yb, 1)

            for i in range(8):
                estep(i, i % 4, i // 4, up=i >= 1, down=i >= 3, dest=i >= 2)
            with v.Fori(1, MAXT // 8) as q:
                for u in range(8):
                    estep(8 * q + u, u % 4, 2 * q + u // 4)
            for i in range(MAXT // 8 * 8, MAXT + 3):
                estep(i, i % 4, i // 4, new=i < MAXT, up=i - 1 < MAXT, dest=i - 2 < MAXT)

            def late_hidden(j):
                v.wait_ge(s_th, NOW + j + 1)
                v.wait_ge(s_u, NOW + j + 1)
                if j < 2:
                    v.wait_ge(s_yo, MAXT)
                else:
                    v.wait_ge(s_ht, NOW + j - 1)
                v.tensor_tensor(late_hid[j], late_sil[j], psPT[:, :], ALU.mult).then_inc(s_h, 1)

            def late_add_z(j):
                v.wait_ge(s_z, NOW + j + 1)
                v.tensor_tensor(xt(LATE[j]), late_ps_z[j][:, 0:D], xt(LATE[j]), ALU.add).then_inc(s_zd, 1)

            def combine(c):
                v.wait_ge(s_c1, c + 1)
                v.tensor_tensor(x_all[:, 4 * c:4 * c + 4, :], x_all[:, 4 * c:4 * c + 4, :], comb(c)[:, 1], ALU.add).then_inc(s_c2, 1)

            late_hidden(0)
            late_lo(1)
            late_lo(2)
            lo_hT(NOW + 1)
            late_hidden(1)
            late_add_z(0)
            combine(0)
            lo_hT(NOW + 2)
            late_hidden(2)
            combine(1)
            late_add_z(1)
            lo_hT(NOW + 3)
            combine(2)
            v.wait_ge(s_last[0], 16)
            v.wait_ge(s_zd, NT - 1)
            v.tensor_tensor(x_all[:, 12:14, :], x_all[:, 12:14, :], comb(3)[:, 0, 0:2], ALU.add).then_inc(s_c3, 1)
            v.wait_ge(s_c1, 4)
            late_add_z(2)
            v.wait_ge(s_c3, 1)
            v.wait_ge(s_last[1], 16)
            v.tensor_tensor(x_all[:, 12:14, :], x_all[:, 12:14, :], comb(3)[:, 1, 0:2], ALU.add).then_inc(s_c2, 1)
            v.wait_ge(s_zd, NT)
            v.tensor_tensor(x_all[:, 14:16, :], x_all[:, 14:16, :], comb(3)[:, 1, 2:4], ALU.add).then_inc(s_c2, 1)


        @block.gpsimd
        def _(g):
            made = [0]

            def make(ins):
                made[0] += 1
                return ins.then_inc(s_const, 1)

            make(g.memset(nhalf[:], -0.5))
            make(g.memset(ident[:], 0.0))
            make(g.memset(ones[:], 1.0))
            make(g.memset(earlier[:], 0.0))
            make(g.memset(fill_blk[:], 0.0))
            make(g.memset(upto[:], 0.0))
            make(g.memset(rows[:, :, D + 1:ROW], 0.0))
            g.wait_ge(s_const, made[0])
            make(g.affine_select(out=ident[:], in_=ident[:], compare_op=ALU.not_equal, fill=1.0, base=0, pattern=[[-1, P]], channel_multiplier=1))
            make(g.affine_select(out=earlier[:], in_=earlier[:], compare_op=ALU.is_ge, fill=1.0, base=0, pattern=[[-1, P]], channel_multiplier=1))
            make(g.affine_select(out=upto[:], in_=upto[:], compare_op=ALU.is_gt, fill=1.0, base=0, pattern=[[-1, NE], [1, NE]], channel_multiplier=0))
            make(g.iota(fill_blk[:, D:D + 1].bitcast(I32), pattern=[[0, 1]], base=SKIP, channel_multiplier=1))
            make(g.iota(dest_i[:], pattern=[[S, B], [1, TB], [T, TOP]], base=0, channel_multiplier=TB))
            make(g.iota(desc[:], pattern=[[0, 2], [-1, NE]], base=NE, channel_multiplier=0, allow_small_or_imprecise_dtypes=True))
            make(g.iota(next_row[:], pattern=[[REGION, NE]], base=0, channel_multiplier=0, allow_small_or_imprecise_dtypes=True))
            make(g.iota(base_row[:], pattern=[[REGION, NE]], base=0, channel_multiplier=0, allow_small_or_imprecise_dtypes=True))
            make(g.iota(m128[:], pattern=[[0, NE], [P, NT]], base=0, channel_multiplier=0, allow_small_or_imprecise_dtypes=True))
            make(g.iota(tile_no[:, :, :], pattern=[[1, MAXT], [0, NE]], base=0, channel_multiplier=0, allow_small_or_imprecise_dtypes=True))
            assert made[0] == NCONST

            def rstd1_of(a, b, n):
                g.wait_ge(s_mv1, b)
                g.tensor_scalar(ve1[:, a:b], mv1[:, a:b, 1], EPS, None, ALU.add).then_inc(s_ve1, 1)
                g.wait_ge(s_ve1, n)
                g.tensor_tensor(rstd1[:, a:b], ve1[:, a:b], nhalf[:, 0:1].to_broadcast([P, b - a]), ALU.pow).then_inc(s_rs1, 1)

            def rstd2_of(n):
                g.wait_ge(s_mv2, n)
                if not isinstance(n, int):
                    apart(g, s_pg)
                g.tensor_scalar(ve2[:], mv2[:, 1:2], EPS, None, ALU.add).then_inc(s_ve2, 1)
                g.wait_ge(s_ve2, n)
                g.tensor_tensor(rstd2[:], ve2[:], nhalf[:], ALU.pow).then_inc(s_rs2, 1)

            def step(i, u, p, norm=True):
                if norm:
                    rstd2_of(i)
                if u == 0 and past(i, 4):
                    if not past_int(i, 15):
                        split_lo(p - 2)
                    dests(p - 1, i - 4)
                if u == 1 and past(i, 5):
                    scatter(p - 1)

            def dests(n, t):
                if past(n, 2):
                    for k in range(4):
                        g.wait_ge(s_sc[k], 16 * (n - 1))
                    apart(g, s_pg)
                d = dest_i[:, t:t + 2, :] if isinstance(t, int) else dest_i[:, bass.ds(t, 2), :]
                g.tensor_copy(rows[:, :, D].bitcast(I32), d.rearrange("p a s -> p (a s)")).then_inc(s_dst, 1)

            def scatter(n, tiles=range(2)):
                g.wait_ge(s_pos, n)
                g.wait_ge(s_dst, n)
                if not isinstance(n, int):
                    g.wait_ge(s_row, 4 * n)
                    apart(g, s_pg)
                for t in tiles:
                    for s in range(TOP):
                        k = 2 * t + s
                        if isinstance(n, int):
                            g.wait_ge(s_row, 4 * (n - 1) + k + 1)
                        g.indirect_dma_start(out=sorted_rows, out_offset=bass.IndirectOffsetOnAxis(ap=pos_i[:, s, t:t + 1], axis=0),
                                             in_=rows[:, k, :], in_offset=None).then_inc(s_sc[k], 16)

            def split_lo(e):
                for k, (wh, wl, raw) in enumerate(((w13_hi, w13_lo, w13_raw()), (w2_hi, w2_lo, w2_raw()))):
                    g.wait_ge(s_ehi, 2 * e + 1 + k)
                    g.tensor_tensor(flat(wl, e), raw, flat(wh, e).bitcast(F32), ALU.subtract).then_inc(s_elo, 1)

            rstd1_of(0, 2, 1)
            g.wait_ge(s_slo, 2)
            setup_lo(g, 2)
            rstd1_of(2, TB, 2)
            setup_lo(g, 3)
            step(1, 1, 0)
            setup_lo(g, 4)
            step(2, 0, 1)
            rstd1_of(TB, NT, 3)
            for i in range(3, 6):
                step(i, i % 2, i // 2)
            with g.Fori(3, NT // 2 - 1) as p:
                for u in range(2):
                    step(2 * p + u, u, p)
            step(14, 0, 7)
            rstd2_of(15)
            scatter(6, [0])
            rstd2_of(NT)
            scatter(6, [1])
            dests(7, 12)
            scatter(7)
            dests(NT // 2, NT - 2)
            scatter(NT // 2)
            g.wait_ge(s_lhi, 2)
            g.tensor_tensor(flat(w2_lo, 6), w2_raw(), flat(w2_hi, 6).bitcast(F32), ALU.subtract).then_inc(s_llo, 1)
            g.wait_ge(s_lhi, 5)
            g.tensor_tensor(flat(w2_lo, 7), w2_raw7, flat(w2_hi, 7).bitcast(F32), ALU.subtract).then_inc(s_llo, 1)

            def ytail(j, k, n, s):
                g.wait_ge(s_yb, n)
                if s is not None:
                    g.wait_ge(s_ys[k], s)
                g.tensor_tensor(yout[k], yb[:, k % 2, :], u13[k][:, H:2 * H], ALU.mult).then_inc(s_yo, 1)
                g.wait_ge(s_yo, n)
                apart(g, s_pg)
                g.indirect_dma_start(out=expert_out, out_offset=bass.IndirectOffsetOnAxis(ap=dest_row[:, k:k + 1], axis=0),
                                     in_=yout[k], in_offset=None, bounds_check=TOP * T - 1, oob_is_err=False).then_inc(s_ys[k], 16)

            for j in range(4):
                ytail(j, j, j + 1, None)
            with g.Fori(1, 9) as q:
                for k in range(4):
                    ytail(None, k, 4 * q + k + 1, 16 * q)
            for j in range(36, MAXT):
                ytail(j, j % 4, j + 1, 16 * (j // 4))

            g.wait_ge(s_zd, NOW)
            for c in range(3):
                g.wait_ge(s_c[c], 32)
                g.tensor_tensor(x_all[:, 4 * c:4 * c + 4, :], x_all[:, 4 * c:4 * c + 4, :], comb(c)[:, 0], ALU.add).then_inc(s_c1, 1)
            g.wait_ge(s_last[0], 16)
            g.tensor_tensor(x_all[:, 14:16, :], x_all[:, 14:16, :], comb(3)[:, 0, 2:4], ALU.add).then_inc(s_c1, 1)


def kernel(x, ctx_1024, mask_BxSxS2_bk0, L0_xattn_W_attn, L0_ffn_gate_w, L0_ffn_w1, L0_ffn_b1,
           L0_ffn_w2, L0_ffn_b2, L0_ffn_w3, L0_ffn_b3, L0_ffn_sw1, L0_ffn_sw2, L0_ffn_sw3):
    import concourse.bacc as bacc
    import numpy as np
    from concourse.bass_utils import run_bass_kernel_spmd

    w_attn = np.asarray(L0_xattn_W_attn)
    laid = {
        "x": np.asarray(x),
        "enc_t": np.asarray(ctx_1024).transpose(0, 2, 1),
        "mask": np.asarray(mask_BxSxS2_bk0),
        "w_ctx": w_attn[:, :D].T,
        "w_dec": w_attn[:, D:].T,
        "gate_t": np.asarray(L0_ffn_gate_w).T,
        "sw12": np.concatenate([np.asarray(L0_ffn_sw1).T, np.asarray(L0_ffn_sw2).T], axis=1),
        "sw3": np.asarray(L0_ffn_sw3).T,
        "w13": np.concatenate([np.asarray(L0_ffn_w1).transpose(0, 2, 1), np.asarray(L0_ffn_w3).transpose(0, 2, 1)], axis=2),
        "w2": np.asarray(L0_ffn_w2).transpose(0, 2, 1),
        "bias": np.concatenate([np.asarray(L0_ffn_b1), np.asarray(L0_ffn_b3), np.asarray(L0_ffn_b2)], axis=1),
    }
    nc = bacc.Bacc("TRN2", target_bir_lowering=False, num_devices=1)
    arrays = {name: np.ascontiguousarray(a) for name, a in laid.items()}
    args = [nc.dram_tensor(name, a.shape, mybir.dt.from_np(a.dtype), kind="ExternalInput").ap() for name, a in arrays.items()]
    args.append(nc.dram_tensor("out", (B, S, D), F32, kind="ExternalOutput").ap())
    bass_xattn_moe(nc, *args)
    r = run_bass_kernel_spmd(nc, [arrays], core_ids=[0])
    return r.results[0]["out"]
```
